# Optimizing a Trainium2 kernel written in Bass

```python
import numpy as np
import jax
import jax.numpy as jnp

def _softmax(x, axis=-1):
    return jax.nn.softmax(x, axis=axis)

def _gelu(x):
    return jax.nn.gelu(x, approximate=True)

def _silu(x):
    return jax.nn.silu(x)

def _sigmoid(x):
    return jax.nn.sigmoid(x)

def _layernorm(x, axis=-1, eps=1e-05):
    m = jnp.mean(x, axis=axis, keepdims=True)
    v = jnp.var(x, axis=axis, keepdims=True)
    return (x - m) / jnp.sqrt(v + eps)

def _scatter_add(tgt, idx, src, axis=0):
    return tgt.at[idx].add(src)

def _segment_sum(src, seg, n):
    return jax.ops.segment_sum(src, seg, n)
kernel_name = 'mk_dlrm_tower_d1_rec_r8_52c200'

def setup_inputs(seed: int=0):
    np.random.seed(seed)
    _w = jnp.asarray

    def _rec_inputs():
        import jax
        import jax.numpy as jnp
        _tk = jax.random.key(seed)
        ids = jnp.stack([jax.random.randint(jax.random.fold_in(_tk, 200 + f), (2048,), 0, v, jnp.int32) for f, v in enumerate([125000, 1000, 1250, 125000, 125000, 1250, 12500, 12500, 1250, 12500, 1250, 12500, 12500, 1000, 12500, 1250, 1000, 12500, 1250, 1250, 1000, 12500, 1250, 1250, 1000, 1250])], axis=1)
        tbl_0 = 0.05 * jax.random.normal(jax.random.fold_in(_tk, 500 + 0), (125000, 64), jnp.float32)
        tbl_1 = 0.05 * jax.random.normal(jax.random.fold_in(_tk, 500 + 1), (1000, 64), jnp.float32)
        tbl_2 = 0.05 * jax.random.normal(jax.random.fold_in(_tk, 500 + 2), (1250, 64), jnp.float32)
        tbl_3 = 0.05 * jax.random.normal(jax.random.fold_in(_tk, 500 + 3), (125000, 64), jnp.float32)
        tbl_4 = 0.05 * jax.random.normal(jax.random.fold_in(_tk, 500 + 4), (125000, 64), jnp.float32)
        tbl_5 = 0.05 * jax.random.normal(jax.random.fold_in(_tk, 500 + 5), (1250, 64), jnp.float32)
        tbl_6 = 0.05 * jax.random.normal(jax.random.fold_in(_tk, 500 + 6), (12500, 64), jnp.float32)
        tbl_7 = 0.05 * jax.random.normal(jax.random.fold_in(_tk, 500 + 7), (12500, 64), jnp.float32)
        tbl_8 = 0.05 * jax.random.normal(jax.random.fold_in(_tk, 500 + 8), (1250, 64), jnp.float32)
        tbl_9 = 0.05 * jax.random.normal(jax.random.fold_in(_tk, 500 + 9), (12500, 64), jnp.float32)
        tbl_10 = 0.05 * jax.random.normal(jax.random.fold_in(_tk, 500 + 10), (1250, 64), jnp.float32)
        tbl_11 = 0.05 * jax.random.normal(jax.random.fold_in(_tk, 500 + 11), (12500, 64), jnp.float32)
        tbl_12 = 0.05 * jax.random.normal(jax.random.fold_in(_tk, 500 + 12), (12500, 64), jnp.float32)
        tbl_13 = 0.05 * jax.random.normal(jax.random.fold_in(_tk, 500 + 13), (1000, 64), jnp.float32)
        tbl_14 = 0.05 * jax.random.normal(jax.random.fold_in(_tk, 500 + 14), (12500, 64), jnp.float32)
        tbl_15 = 0.05 * jax.random.normal(jax.random.fold_in(_tk, 500 + 15), (1250, 64), jnp.float32)
        tbl_16 = 0.05 * jax.random.normal(jax.random.fold_in(_tk, 500 + 16), (1000, 64), jnp.float32)
        tbl_17 = 0.05 * jax.random.normal(jax.random.fold_in(_tk, 500 + 17), (12500, 64), jnp.float32)
        tbl_18 = 0.05 * jax.random.normal(jax.random.fold_in(_tk, 500 + 18), (1250, 64), jnp.float32)
        tbl_19 = 0.05 * jax.random.normal(jax.random.fold_in(_tk, 500 + 19), (1250, 64), jnp.float32)
        tbl_20 = 0.05 * jax.random.normal(jax.random.fold_in(_tk, 500 + 20), (1000, 64), jnp.float32)
        tbl_21 = 0.05 * jax.random.normal(jax.random.fold_in(_tk, 500 + 21), (12500, 64), jnp.float32)
        tbl_22 = 0.05 * jax.random.normal(jax.random.fold_in(_tk, 500 + 22), (1250, 64), jnp.float32)
        tbl_23 = 0.05 * jax.random.normal(jax.random.fold_in(_tk, 500 + 23), (1250, 64), jnp.float32)
        tbl_24 = 0.05 * jax.random.normal(jax.random.fold_in(_tk, 500 + 24), (1000, 64), jnp.float32)
        tbl_25 = 0.05 * jax.random.normal(jax.random.fold_in(_tk, 500 + 25), (1250, 64), jnp.float32)
        _rk = jax.random.fold_in(_tk, 7)
        r_dense_t = 7.22013e-05 + 1.00017 * jax.random.normal(jax.random.fold_in(_rk, 101), (2048, 256), jnp.float32)
        W_top1 = 0.0360844 * jax.random.normal(jax.random.fold_in(_tk, 801), (768, 512), jnp.float32)
        W_top2 = 0.0441942 * jax.random.normal(jax.random.fold_in(_tk, 802), (512, 256), jnp.float32)
        W_top3 = 0.0625 * jax.random.normal(jax.random.fold_in(_tk, 803), (256, 1), jnp.float32)
        b_top1 = jnp.zeros((512,), jnp.float32)
        b_top2 = jnp.zeros((256,), jnp.float32)
        return (r_dense_t, ids, tbl_0, tbl_1, tbl_2, tbl_3, tbl_4, tbl_5, tbl_6, tbl_7, tbl_8, tbl_9, tbl_10, tbl_11, tbl_12, tbl_13, tbl_14, tbl_15, tbl_16, tbl_17, tbl_18, tbl_19, tbl_20, tbl_21, tbl_22, tbl_23, tbl_24, tbl_25, W_top1, b_top1, W_top2, b_top2, W_top3)
    r_dense_t, ids, tbl_0, tbl_1, tbl_2, tbl_3, tbl_4, tbl_5, tbl_6, tbl_7, tbl_8, tbl_9, tbl_10, tbl_11, tbl_12, tbl_13, tbl_14, tbl_15, tbl_16, tbl_17, tbl_18, tbl_19, tbl_20, tbl_21, tbl_22, tbl_23, tbl_24, tbl_25, W_top1, b_top1, W_top2, b_top2, W_top3 = _rec_inputs()

    def _L0_rec_setup():
        import jax, jax.numpy as jnp
        import numpy as np
        EPS = 1e-05
        NI = 33
        TRIL_I, TRIL_J = np.tril_indices(NI, k=-1)

        def layer_norm(x, g, b):
            m = jnp.mean(x, axis=-1, keepdims=True)
            v = jnp.mean(jnp.square(x - m), axis=-1, keepdims=True)
            return (x - m) * jax.lax.rsqrt(v + EPS) * g + b
        key = jax.random.key(seed)
        ks = jax.random.split(key, 8)
        B, D_DENSE, N_SP, D_SP = (4096, 256, 26, 64)
        E, PROJ, MAXD, NFLAT = (128, 32, 512, 528)
        dense_t = jax.random.normal(ks[0], (B, D_DENSE), dtype=jnp.float32)
        sparse_t = jax.random.normal(ks[1], (B, N_SP, D_SP), dtype=jnp.float32)
        Wd = jax.random.normal(ks[2], (E, D_DENSE), dtype=jnp.float32) / np.sqrt(D_DENSE)
        Ws = jax.random.normal(ks[3], (E, D_SP), dtype=jnp.float32) / np.sqrt(D_SP)
        Wsi = jax.random.normal(ks[4], (PROJ, N_SP), dtype=jnp.float32) / np.sqrt(N_SP)
        Wl = jax.random.normal(ks[5], (MAXD, NFLAT), dtype=jnp.float32) / np.sqrt(NFLAT)
        gd = jnp.ones((E,), jnp.float32)
        bd = jnp.zeros((E,), jnp.float32)
        gs = jnp.ones((E,), jnp.float32)
        bs = jnp.zeros((E,), jnp.float32)
        gsi = jnp.ones((PROJ,), jnp.float32)
        bsi = jnp.zeros((PROJ,), jnp.float32)
        gl = jnp.ones((MAXD,), jnp.float32)
        bl = jnp.zeros((MAXD,), jnp.float32)
        return {'dense_t': dense_t, 'sparse_t': sparse_t, 'Wd': Wd, 'gd': gd, 'bd': bd, 'Ws': Ws, 'gs': gs, 'bs': bs, 'Wsi': Wsi, 'gsi': gsi, 'bsi': bsi, 'Wl': Wl, 'gl': gl, 'bl': bl, 'dims_in_use': 384}
    _L0_rec_all = _L0_rec_setup()
    _L0_rec_in = {k: v for k, v in _L0_rec_all.items() if k in ('Wd', 'gd', 'bd', 'Ws', 'gs', 'bs', 'Wsi', 'gsi', 'bsi', 'Wl', 'gl', 'bl')}
    del _L0_rec_all
    return {'r_dense_t': r_dense_t, 'ids': ids, 'tbl_0': tbl_0, 'tbl_1': tbl_1, 'tbl_2': tbl_2, 'tbl_3': tbl_3, 'tbl_4': tbl_4, 'tbl_5': tbl_5, 'tbl_6': tbl_6, 'tbl_7': tbl_7, 'tbl_8': tbl_8, 'tbl_9': tbl_9, 'tbl_10': tbl_10, 'tbl_11': tbl_11, 'tbl_12': tbl_12, 'tbl_13': tbl_13, 'tbl_14': tbl_14, 'tbl_15': tbl_15, 'tbl_16': tbl_16, 'tbl_17': tbl_17, 'tbl_18': tbl_18, 'tbl_19': tbl_19, 'tbl_20': tbl_20, 'tbl_21': tbl_21, 'tbl_22': tbl_22, 'tbl_23': tbl_23, 'tbl_24': tbl_24, 'tbl_25': tbl_25, 'W_top1': W_top1, 'b_top1': b_top1, 'W_top2': W_top2, 'b_top2': b_top2, 'W_top3': W_top3, 'L0_rec_Wd': _L0_rec_in['Wd'], 'L0_rec_gd': _L0_rec_in['gd'], 'L0_rec_bd': _L0_rec_in['bd'], 'L0_rec_Ws': _L0_rec_in['Ws'], 'L0_rec_gs': _L0_rec_in['gs'], 'L0_rec_bs': _L0_rec_in['bs'], 'L0_rec_Wsi': _L0_rec_in['Wsi'], 'L0_rec_gsi': _L0_rec_in['gsi'], 'L0_rec_bsi': _L0_rec_in['bsi'], 'L0_rec_Wl': _L0_rec_in['Wl'], 'L0_rec_gl': _L0_rec_in['gl'], 'L0_rec_bl': _L0_rec_in['bl']}

def reference(r_dense_t, ids, tbl_0, tbl_1, tbl_2, tbl_3, tbl_4, tbl_5, tbl_6, tbl_7, tbl_8, tbl_9, tbl_10, tbl_11, tbl_12, tbl_13, tbl_14, tbl_15, tbl_16, tbl_17, tbl_18, tbl_19, tbl_20, tbl_21, tbl_22, tbl_23, tbl_24, tbl_25, W_top1, b_top1, W_top2, b_top2, W_top3, L0_rec_Wd, L0_rec_gd, L0_rec_bd, L0_rec_Ws, L0_rec_gs, L0_rec_bs, L0_rec_Wsi, L0_rec_gsi, L0_rec_bsi, L0_rec_Wl, L0_rec_gl, L0_rec_bl):
    import jax
    import jax.numpy as jnp

    def _L0_rec_ref(dense_t, sparse_t, Wd, gd, bd, Ws, gs, bs, Wsi, gsi, bsi, Wl, gl, bl, dims_in_use):
        import jax, jax.numpy as jnp
        import numpy as np
        EPS = 1e-05
        NI = 33
        TRIL_I, TRIL_J = np.tril_indices(NI, k=-1)

        def layer_norm(x, g, b):
            m = jnp.mean(x, axis=-1, keepdims=True)
            v = jnp.mean(jnp.square(x - m), axis=-1, keepdims=True)
            return (x - m) * jax.lax.rsqrt(v + EPS) * g + b
        x = layer_norm(dense_t @ Wd.T, gd, bd)
        y = layer_norm(jnp.einsum('bnd,ed->bne', sparse_t, Ws), gs, bs)
        y = jnp.einsum('bne,pn->bep', y, Wsi)
        y = layer_norm(y, gsi, bsi)
        y = jnp.swapaxes(y, 1, 2)
        T = jnp.concatenate([x[:, None, :], y], axis=1)
        Z = jnp.einsum('bnd,bmd->bnm', T, T)
        Zflat = Z[:, TRIL_I, TRIL_J]
        out = layer_norm(Zflat @ Wl.T, gl, bl)
        maxd = out.shape[-1]
        mask = (jnp.arange(maxd) < dims_in_use).astype(out.dtype)
        return out * mask
    e = jnp.stack([tbl_0[ids[:, 0]], tbl_1[ids[:, 1]], tbl_2[ids[:, 2]], tbl_3[ids[:, 3]], tbl_4[ids[:, 4]], tbl_5[ids[:, 5]], tbl_6[ids[:, 6]], tbl_7[ids[:, 7]], tbl_8[ids[:, 8]], tbl_9[ids[:, 9]], tbl_10[ids[:, 10]], tbl_11[ids[:, 11]], tbl_12[ids[:, 12]], tbl_13[ids[:, 13]], tbl_14[ids[:, 14]], tbl_15[ids[:, 15]], tbl_16[ids[:, 16]], tbl_17[ids[:, 17]], tbl_18[ids[:, 18]], tbl_19[ids[:, 19]], tbl_20[ids[:, 20]], tbl_21[ids[:, 21]], tbl_22[ids[:, 22]], tbl_23[ids[:, 23]], tbl_24[ids[:, 24]], tbl_25[ids[:, 25]]], axis=1)
    z = _L0_rec_ref(r_dense_t, e, L0_rec_Wd, L0_rec_gd, L0_rec_bd, L0_rec_Ws, L0_rec_gs, L0_rec_bs, L0_rec_Wsi, L0_rec_gsi, L0_rec_bsi, L0_rec_Wl, L0_rec_gl, L0_rec_bl, 384)
    z = z.reshape(z.shape[0], -1)
    h = jnp.concatenate([z, r_dense_t], axis=1)
    h = jnp.maximum(h @ W_top1 + b_top1, 0.0)
    h = jnp.maximum(h @ W_top2 + b_top2, 0.0)
    y = h @ W_top3
    return y

_drawn_inputs = setup_inputs


def setup_inputs(seed=0):
    import zlib

    import numpy as np

    out = dict(_drawn_inputs(seed))
    spreads = {'b_top1': (0.0, 0.1),
     'b_top2': (0.0, 0.1),
     'L0_rec_gd': (1.0, 0.6),
     'L0_rec_bd': (0.0, 0.8),
     'L0_rec_gs': (1.0, 0.6),
     'L0_rec_bs': (0.0, 0.1),
     'L0_rec_gsi': (1.0, 0.2),
     'L0_rec_bsi': (0.0, 0.1),
     'L0_rec_gl': (1.0, 0.2),
     'L0_rec_bl': (0.0, 0.1)}
    factors = {}
    for name, (base, spread) in spreads.items():
        noise = np.random.default_rng([zlib.crc32(name.encode()), seed]).standard_normal(out[name].shape)
        drawn = base * np.exp(spread * noise) if base else spread * noise
        out[name] = jnp.asarray(drawn.astype(out[name].dtype))
    for name, factor in factors.items():
        out[name] = (out[name] * factor).astype(out[name].dtype)
    return out
```

```python
from contextlib import ExitStack

import concourse.bass as bass
from concourse import mybir

P = 128
ALU = mybir.AluOpType
ACT = mybir.ActivationFunctionType
F32 = mybir.dt.float32
AX_X = mybir.AxisListType.X
EPS = 1e-5

CREDIT = {
    "transposed": 8, "emb_t_ready": 1, "projected": 7, "scaled": 2, "compressed": 16, "var_ready": 2,
    "z_read": 2, "paired": 4, "regrouped_act": 1, "regrouped_dve": 1, "top_read": 1,
}


def dlrm_tower(nc: bass.Bass, ids, tables, dense_t, ident, wd_t, ws_t2, wsi_t4, block_mask, first_block, bs_row,
               gs_rows, gsi_rows, bsi_rows, columns, wl_pairs, w_top1, w_top2, out):
    B, N = ids.shape
    D = tables[0].shape[1]
    E = wd_t.shape[1]
    FD = dense_t.shape[0]
    PR = wsi_t4.shape[1]
    JJ, O = wl_pairs.shape[1:]
    H1, H2 = w_top1.shape[1], w_top2.shape[1]
    FC = FD // P
    Q = P // PR
    QN = Q * N
    G = P // Q
    TILES = B // P
    JT = 4
    SUPER = TILES // JT
    SB = JT * P
    UN = 8
    GU = G // UN
    UR = Q * GU
    NPAIR = N // 2
    TP = 4
    TCH = -(-NPAIR // TP)
    PP = 2
    PCH = -(-NPAIR // PP)
    OC = O // P
    ZC = 3
    H1C, H2C = H1 // P, H2 // P
    TOPS = OC + 1 + H1C + H2C + 1
    assert (B, N, D, E, PR, O) == (2048, 26, 64, 128, 32, 512) and JJ * Q == PR

    scratch = [nc.dram_tensor(f"normed_dram{s}", (P * N, E), F32, kind="Internal").ap() for s in range(2)]

    with ExitStack() as ctx:
        def sb(name, shape, dt=F32):
            return ctx.enter_context(nc.sbuf_tensor(name, shape, dt))

        def psum(name, shape):
            return ctx.enter_context(nc.psum_tensor(name, shape, F32))

        def sem(name):
            return ctx.enter_context(nc.semaphore(name))

        ident_sb = sb("ident_sb", [P, P])
        ones = sb("ones", [P, P])
        eps = sb("eps", [P, 1])
        wd = sb("wd", [P, FC, E])
        ws2 = sb("ws2", [P, E])
        ws_block = sb("ws_block", [P, 2 * E])
        wsi4 = sb("wsi4", [QN, PR])
        wsi_c = sb("wsi_c", [QN, Q, PR])
        mask = sb("mask", [QN, Q])
        first = sb("first", [QN, 1])
        wsi_block = sb("wsi_block", [QN + 1, P])
        sum_row = sb("sum_row", [1, P])
        gs_b = sb("gs_b", [P, E])
        gsi_b = sb("gsi_b", [P, PR])
        bsi_b = sb("bsi_b", [P, PR])
        cols = sb("cols", [P, columns.shape[1]])
        wl = sb("wl", [P, JJ, O])
        w1 = sb("w1", [P, ZC + FC, H1])
        w2 = sb("w2", [P, H1C, H2])
        dense = sb("dense", [P, FC, B])
        x_all = sb("x_all", [P, B])
        means = sb("means", [P, FC + 2 + JJ])
        at = 0
        col = {}
        for name, k in (("gd", 1), ("bd", 1), ("gl", OC), ("bl", OC), ("b1", H1C), ("b2", H2C), ("w3", H2C)):
            col[name] = [cols[:, at + c:at + c + 1] for c in range(k)]
            at += k

        idx = [sb(f"idx{s}", [P, N], ids.dtype) for s in range(2)]
        emb = [sb(f"emb{s}", [P, N * D]) for s in range(2)]
        emb_t = [sb(f"emb_t{s}", [P, TP * P]) for s in range(2)]
        junk = [sb(f"junk{s}", [P, 2 * PP, E]) for s in range(2)]
        proj_ss = [sb(f"proj_ss{s}", [P, 2 * PP]) for s in range(2)]
        proj_sd = [sb(f"proj_sd{s}", [P, 2 * PP]) for s in range(2)]
        proj_rs = [sb(f"proj_rs{s}", [P, 2 * PP]) for s in range(2)]
        normed = [sb(f"normed{s}", [P, N, E]) for s in range(2)]
        by_group = [sb(f"by_group{s}", [QN + 1, G, E]) for s in range(2)]
        z_sq = [sb(f"z_sq{s}", [P, UR, PR]) for s in range(2)]
        z_var = [sb(f"z_var{s}", [P, UR]) for s in range(2)]
        z_sd = [sb(f"z_sd{s}", [P, UR]) for s in range(2)]
        z_rs = [sb(f"z_rs{s}", [P, UR]) for s in range(2)]
        z_n = [sb(f"z_n{s}", [P, UR, PR]) for s in range(2)]
        items = [sb(f"items{s}", [P, UR, PR + 1]) for s in range(4)]
        pairs = sb("pairs", [P, JJ, SB])
        pair_c = sb("pair_c", [P, OC, SB])
        pair_sq = sb("pair_sq", [P, OC, SB])
        wide_sd = sb("wide_sd", [P, SB])
        wide_rs = sb("wide_rs", [P, SB])
        hidden0 = sb("hidden0", [P, ZC, SB])
        hidden1 = pair_sq
        hidden2 = pair_c
        y_row = sb("y_row", [1, B])

        emb_t_ps = psum("emb_t_ps", [P, TP * P])
        proj_ps = [psum(f"proj_ps{s}", [P, 2 * PP * E]) for s in range(2)]
        z_ps = [psum(f"z_ps{s}", [P, UR, PR]) for s in range(2)]
        gram_ps = [psum(f"gram_ps{s}", [P, G // 2, PR]) for s in range(2)]
        top_ps = psum("top_ps", [P, SB])
        top_bank = [top_ps[:, :]] + [g[:, :, :].rearrange("p a b -> p (a b)") for g in gram_ps]

        weights_in = sem("weights_in")
        late_in = sem("late_in")
        bias_row_in = sem("bias_row_in")
        consts_set = sem("consts_set")
        prep_done = sem("prep_done")
        prep_read = sem("prep_read")
        centred = sem("centred")
        x_scaled = sem("x_scaled")
        ids_in = [sem(f"ids_in{s}") for s in range(2)]
        gathered = [sem(f"gathered{s}") for s in range(2)]
        stored = [sem(f"stored{s}") for s in range(2)]
        loaded = [sem(f"loaded{s}") for s in range(2)]
        transposed = sem("transposed")
        emb_t_ready = sem("emb_t_ready")
        projected = sem("projected")
        proj_sq = sem("proj_sq")
        proj_std = sem("proj_std")
        proj_rstd = sem("proj_rstd")
        scaled = sem("scaled")
        compressed = sem("compressed")
        squared = sem("squared")
        var_ready = sem("var_ready")
        z_std = sem("z_std")
        z_rstd = sem("z_rstd")
        z_read = sem("z_read")
        z_scaled = sem("z_scaled")
        items_ready = sem("items_ready")
        paired = sem("paired")
        regrouped_act = sem("regrouped_act")
        regrouped_dve = sem("regrouped_dve")
        top_done = sem("top_done")
        top_read = sem("top_read")
        hidden0_step = sem("hidden0_step")
        pool_turn = sem("pool_turn")
        y_out = sem("y_out")

        C = CREDIT
        block = ctx.enter_context(nc.Block())

        @block.sync
        def _(sp):
            ids_v = ids.rearrange("(t p) n -> t p n", p=P)

            def load_ids(t, s):
                sp.dma_start(idx[s][:, :], ids_v[bass.ds(t, 1), :, :].rearrange("a p n -> (a p) n")).then_inc(ids_in[s], 16)

            load_ids(0, 0)
            load_ids(1, 1)
            for s in range(2):
                sp.sem_inc(stored[s], 16)
            sp.dma_start(ws2[:, :], ws_t2).then_inc(weights_in, 16)
            sp.dma_start(ident_sb[:, :], ident).then_inc(weights_in, 16)
            sp.dma_start(wd[:, :, :], wd_t.rearrange("(c p) e -> p c e", p=P)).then_inc(weights_in, 16)
            sp.dma_start(wsi4[:, :], wsi_t4).then_inc(weights_in, 16)
            sp.dma_start(mask[:, :], block_mask).then_inc(weights_in, 16)
            sp.dma_start(first[:, :], first_block).then_inc(weights_in, 16)
            sp.dma_start(gs_b[:, :], gs_rows).then_inc(weights_in, 16)
            sp.dma_start(gsi_b[:, :], gsi_rows).then_inc(weights_in, 16)
            sp.dma_start(bsi_b[:, :], bsi_rows).then_inc(weights_in, 16)
            sp.dma_start(cols[:, :], columns).then_inc(weights_in, 16)
            sp.dma_start(dense[:, :, :], dense_t.rearrange("(c p) b -> p c b", p=P)).then_inc(weights_in, 16)
            for s in range(2):
                sp.dma_start(by_group[s][QN:QN + 1, :, :], bs_row.rearrange("(a g) e -> a g e", a=1)).then_inc(bias_row_in, 16)
            sp.dma_start(wl[:, :, :], wl_pairs).then_inc(late_in, 16)
            sp.dma_start(w1[:, 0:ZC, :], w_top1[0:ZC * P, :].rearrange("(c p) h -> p c h", p=P)).then_inc(late_in, 16)
            sp.dma_start(w1[:, ZC:ZC + FC, :], w_top1[O:O + FD, :].rearrange("(c p) h -> p c h", p=P)).then_inc(late_in, 16)
            sp.dma_start(w2[:, :, :], w_top2.rearrange("(c p) h -> p c h", p=P)).then_inc(late_in, 16)
            sp.wait_ge(prep_read, 1)
            sp.dma_start(wsi_block[QN:QN + 1, :], sum_row[0:1, :]).then_inc(bias_row_in, 16)

            def tile(i, j, more):
                t, s, k = JT * i + j, j % 2, 2 * i + j // 2
                if more:
                    sp.wait_ge(gathered[s], 16 * N * (k + 1))
                    load_ids(t + 2, s)
                sp.wait_ge(scaled, C["scaled"] + PCH * (t + 1))
                sp.dma_start(scratch[s].rearrange("(p n) e -> p (n e)", n=N),
                             normed[s][:, :, :].rearrange("p n e -> p (n e)")).then_inc(stored[s], 16)
                sp.wait_ge(stored[s], 16 * (k + 2))
                sp.wait_ge(compressed, C["compressed"] + UN * (t - 1))
                sp.dma_start(by_group[s][0:QN, :, :],
                             scratch[s].rearrange("(g r) e -> r g e", r=QN)).then_inc(loaded[s], 16)

            with sp.Fori(0, SUPER - 1) as i:
                for j in range(JT):
                    tile(i, j, True)
            for j in range(JT):
                tile(SUPER - 1, j, j < 2)

        @block.gpsimd
        def _(pool):
            with pool.Fori(0, SUPER) as i:
                for j in range(JT):
                    t, s, k = JT * i + j, j % 2, 2 * i + j // 2
                    pool.wait_ge(ids_in[s], 16 * (k + 1))
                    pool.wait_ge(transposed, C["transposed"] + TCH * (t - 1))
                    pool.sem_inc(pool_turn, 1)
                    for n in range(N):
                        pool.indirect_dma_start(
                            emb[s][:, D * n:D * (n + 1)], None, tables[n][:, :],
                            bass.IndirectOffsetOnAxis(ap=idx[s][:, n:n + 1], axis=0)).then_inc(gathered[s], 16)

        ORDER = [("z", 0), ("t", 0), ("z", 1), ("p", 0), ("p", 1), ("t", 1), ("g", 0), ("z", 2), ("p", 2),
                 ("g", 1), ("z", 3), ("p", 3), ("t", 2), ("g", 2), ("z", 4), ("p", 4), ("g", 3), ("z", 5),
                 ("t", 3), ("g", 4), ("z", 6), ("g", 5), ("z", 7), ("p", 5), ("g", 6), ("p", 6), ("g", 7)]
        AHEAD = [x for x in ORDER if x[0] in "tp"]

        def pairs_in(chunk, size):
            return min(size, NPAIR - chunk * size)

        def regroup_block(j, h, q, jg):
            dst = pairs[PR * jg:PR * (jg + 1), :, P * j + P // 2 * h + q:P * j + P // 2 * (h + 1):Q]
            src = gram_ps[h][PR * q:PR * (q + 1), :, JJ * jg:JJ * (jg + 1)].rearrange("p g j -> p j g")
            return dst, src

        @block.tensor
        def _(pe):
            for name, s in (("transposed", transposed), ("projected", projected), ("compressed", compressed),
                            ("paired", paired)):
                pe.sem_inc(s, C[name])

            def transpose(t, j, c):
                if c == 0:
                    pe.wait_ge(gathered[j % 2], 8 * N * (t - j % 2) + 16 * N)
                pe.wait_ge(emb_t_ready, C["emb_t_ready"] + TCH * t + c)
                for a in range(pairs_in(c, TP)):
                    at = 2 * D * (TP * c + a)
                    last = pe.transpose(emb_t_ps[:, P * a:P * (a + 1)], emb[j % 2][:, at:at + 2 * D], ident_sb[:, :])
                last.then_inc(transposed, 1)

            def project(t, j, c):
                if c % 2 == 0:
                    pe.wait_ge(emb_t_ready, C["emb_t_ready"] + TCH * t + c // 2 + 1)
                pe.wait_ge(scaled, PCH * t + c + 1)
                for a in range(pairs_in(c, PP)):
                    at = P * (PP * (c % 2) + a)
                    last = pe.matmul(proj_ps[(j + c) % 2][:, 2 * E * a:2 * E * (a + 1)], emb_t[c // 2 % 2][:, at:at + P],
                                     ws_block[:, :], start=True, stop=True)
                last.then_inc(projected, 1)

            def compress(t, j, k, m):
                if m == 0:
                    pe.wait_ge(loaded[j % 2], 16 * (k + 1))
                pe.wait_ge(z_read, UN * t + m + 1)
                for a in range(GU):
                    last = pe.matmul(z_ps[m % 2][:, Q * a:Q * (a + 1), :], by_group[j % 2][:, GU * m + a, :],
                                     wsi_block[:, :], start=True, stop=True)
                last.then_inc(compressed, 1)

            def pair(t, m):
                h = m // (UN // 2)
                if m % (UN // 2) == 0:
                    pe.wait_ge(regrouped_dve if h else regrouped_act, t + 1)
                pe.wait_ge(items_ready, UN * t + m + 1)
                it = items[m % 4]
                for a in range(GU):
                    g = GU * (m % (UN // 2)) + a
                    for q in range(Q):
                        r = Q * a + q
                        last = pe.matmul(gram_ps[h][PR * q:PR * (q + 1), g, :], it[:, r, 1:PR + 1], it[:, r, 0:PR],
                                         start=True, stop=True)
                last.then_inc(paired, 1)

            def ahead(t, j):
                for kind, c in AHEAD:
                    transpose(t, j, c) if kind == "t" else project(t, j, c)

            pe.wait_ge(consts_set, 4)
            pe.matmul(top_ps[0:1, 0:P], first[:, :], wsi_c[:, :, :].rearrange("r q p -> r (q p)"),
                      start=True, stop=True).then_inc(prep_done, 1)
            ahead(0, 0)
            ahead(1, 1)
            for blk in range(SUPER):
                pe.wait_ge(prep_read, 2 * blk + 1)
                for c in range(FC):
                    last = pe.matmul(top_ps[:, :], wd[:, c, :], dense[:, c, SB * blk:SB * (blk + 1)],
                                     start=c == 0, stop=c == FC - 1)
                last.then_inc(prep_done, 1)
                pe.wait_ge(prep_read, 2 * blk + 2)
                pe.matmul(top_ps[:, :], ones[:, :], pair_sq[:, 0, :], start=True, stop=True).then_inc(prep_done, 1)

            pe.wait_ge(bias_row_in, 48)
            pe.wait_ge(prep_read, 2 * SUPER + 1)

            def tile(i, j, more):
                t, k = JT * i + j, 2 * i + j // 2
                for kind, c in ORDER:
                    if kind == "z":
                        compress(t, j, k, c)
                    elif kind == "g":
                        pair(t, c)
                    elif more and kind == "t":
                        transpose(t + 2, j, c)
                    elif more and kind == "p":
                        project(t + 2, j, c)

            def top(i):
                def begin(k):
                    if k >= 3:
                        pe.wait_ge(top_read, C["top_read"] + TOPS * i + k - 2)
                    return top_bank[k % 3]

                for oc in range(OC):
                    if oc == 0:
                        pe.wait_ge(regrouped_act, C["regrouped_act"] + JT * (i + 1))
                        pe.wait_ge(regrouped_dve, C["regrouped_dve"] + JT * (i + 1))
                    dst = begin(oc)
                    for jj in range(JJ):
                        last = pe.matmul(dst, wl[:, jj, P * oc:P * (oc + 1)], pairs[:, jj, :],
                                         start=jj == 0, stop=jj == JJ - 1)
                    last.then_inc(top_done, 1)
                dst = begin(OC)
                pe.wait_ge(top_read, C["top_read"] + TOPS * i + OC)
                for oc in range(OC):
                    last = pe.matmul(dst, ones[:, :], pair_sq[:, oc, :], start=oc == 0, stop=oc == OC - 1)
                last.then_inc(top_done, 1)
                for h in range(H1C):
                    dst = begin(OC + 1 + h)
                    for c in range(FC):
                        pe.matmul(dst, w1[:, ZC + c, P * h:P * (h + 1)], dense[:, c, bass.ds(SB * i, SB)],
                                  start=c == 0, stop=False)
                    for c in range(ZC):
                        if h == 0 and c == 0:
                            pe.wait_ge(hidden0_step, 3 * (i + 1))
                        last = pe.matmul(dst, w1[:, c, P * h:P * (h + 1)], hidden0[:, c, :], start=False, stop=c == ZC - 1)
                    last.then_inc(top_done, 1)
                for h in range(H2C):
                    dst = begin(OC + 1 + H1C + h)
                    pe.wait_ge(top_read, C["top_read"] + TOPS * i + OC + 1 + H1C)
                    for c in range(H1C):
                        last = pe.matmul(dst, w2[:, c, P * h:P * (h + 1)], hidden1[:, c, :],
                                         start=c == 0, stop=c == H1C - 1)
                    last.then_inc(top_done, 1)
                dst = begin(TOPS - 1)
                pe.wait_ge(top_read, C["top_read"] + TOPS * i + TOPS - 1)
                for c in range(H2C):
                    last = pe.matmul(dst[0:1, :], col["w3"][c], hidden2[:, c, :], start=c == 0, stop=c == H2C - 1)
                last.then_inc(top_done, 1)
                pe.wait_ge(top_read, C["top_read"] + TOPS * (i + 1))

            pe.wait_ge(late_in, 64)
            pe.wait_ge(consts_set, 6)
            with pe.Fori(0, SUPER - 1) as i:
                for j in range(JT):
                    tile(i, j, True)
                top(i)
            for j in range(JT):
                tile(SUPER - 1, j, j < 2)
            top(SUPER - 1)

        @block.scalar
        def _(act):
            for name, s in (("emb_t_ready", emb_t_ready), ("regrouped_act", regrouped_act), ("top_read", top_read)):
                act.sem_inc(s, C[name])

            def copy_emb_t(t, c):
                act.wait_ge(transposed, C["transposed"] + TCH * t + c + 1)
                before = PCH * t + (2 * c - 2 if c >= 2 else c - 1)
                act.wait_ge(projected, C["projected"] + before)
                w = P * pairs_in(c, TP)
                act.activation(emb_t[c % 2][:, 0:w], emb_t_ps[:, 0:w], ACT.Copy).then_inc(emb_t_ready, 1)

            def square_proj(t, j, c):
                act.wait_ge(projected, C["projected"] + PCH * t + c + 1)
                s = (j + c) % 2
                for a in range(2 * pairs_in(c, PP)):
                    last = act.activation(junk[s][:, a, :], proj_ps[s][:, E * a:E * (a + 1)], ACT.Square,
                                          accum_out=proj_ss[s][:, a:a + 1])
                last.then_inc(proj_sq, 1)

            def std_proj(t, j, c):
                s, w = (j + c) % 2, 2 * pairs_in(c, PP)
                act.wait_ge(proj_sq, PCH * t + c + 1)
                act.activation(proj_sd[s][:, 0:w], proj_ss[s][:, 0:w], ACT.Sqrt, bias=eps[:, :],
                               scale=1.0 / E).then_inc(proj_std, 1)

            def square_z(t, m):
                act.wait_ge(compressed, C["compressed"] + UN * t + m + 1)
                act.wait_ge(var_ready, UN * t + m + 1)
                act.activation(z_sq[m % 2][:, :, :], z_ps[m % 2][:, :, :], ACT.Square).then_inc(squared, 1)

            def std_z(t, m):
                act.wait_ge(var_ready, C["var_ready"] + UN * t + m + 1)
                act.activation(z_sd[m % 2][:, :], z_var[m % 2][:, :], ACT.Sqrt, bias=eps[:, :],
                               scale=1.0 / PR).then_inc(z_std, 1)

            def regroup(t, j, h):
                act.wait_ge(paired, C["paired"] + UN * t + UN // 2 * (h + 1))
                for q in range(Q):
                    for jg in range(Q):
                        last = act.activation(*regroup_block(j, h, q, jg), ACT.Copy)
                last.then_inc(regrouped_act, 1)

            def ahead(t, j):
                waiting = None
                for kind, c in AHEAD:
                    if kind == "t":
                        copy_emb_t(t, c)
                    else:
                        square_proj(t, j, c)
                        std_proj(t, j, c)

            act.wait_ge(consts_set, 3)
            act.wait_ge(prep_done, 1)
            act.activation(sum_row[:, :], top_ps[0:1, 0:P], ACT.Copy).then_inc(prep_read, 1)
            ahead(0, 0)
            ahead(1, 1)
            for blk in range(SUPER):
                act.wait_ge(prep_done, 2 * blk + 2)
                if blk >= 1:
                    act.wait_ge(x_scaled, 4 * blk)
                act.activation(pair_c[:, 0, :], top_ps[:, :], ACT.Copy)
                act.activation(pair_sq[:, 0, :], top_ps[:, :], ACT.Square).then_inc(prep_read, 1)
                act.wait_ge(prep_done, 2 * blk + 3)
                act.activation(wide_sd[:, :], top_ps[:, :], ACT.Sqrt, bias=eps[:, :], scale=1.0 / E).then_inc(prep_read, 1)

            def tile(i, j, more):
                t = JT * i + j
                for kind, c in ORDER:
                    if kind == "z":
                        square_z(t, c)
                        std_z(t, c)
                    elif kind == "g":
                        if c == UN // 2 - 1:
                            regroup(t, j, 0)
                    elif more and kind == "t":
                        copy_emb_t(t + 2, c)
                    elif more and kind == "p":
                        square_proj(t + 2, j, c)
                        std_proj(t + 2, j, c)

            def top(i):
                def ready(k):
                    act.wait_ge(top_done, TOPS * i + k + 1)
                    return top_bank[k % 3]

                for oc in range(OC):
                    src = ready(oc)
                    act.activation(pair_c[:, oc, :], src, ACT.Copy)
                    act.activation(pair_sq[:, oc, :], src, ACT.Square).then_inc(top_read, 1)
                act.activation(wide_sd[:, :], ready(OC), ACT.Sqrt, bias=eps[:, :], scale=1.0 / O).then_inc(top_read, 1)
                for h in range(H1C):
                    act.activation(hidden1[:, h, :], ready(OC + 1 + h), ACT.Relu, bias=col["b1"][h]).then_inc(top_read, 1)
                for h in range(H2C):
                    act.activation(hidden2[:, h, :], ready(OC + 1 + H1C + h), ACT.Relu,
                                   bias=col["b2"][h]).then_inc(top_read, 1)
                act.activation(y_row[0:1, bass.ds(SB * i, SB)], ready(TOPS - 1)[0:1, :], ACT.Copy).then_inc(top_read, 1)

            with act.Fori(0, SUPER - 1) as i:
                for j in range(JT):
                    tile(i, j, True)
                top(i)
            for j in range(JT):
                tile(SUPER - 1, j, j < 2)
            top(SUPER - 1)
            act.wait_ge(top_read, C["top_read"] + TOPS * SUPER)
            act.dma_start(out.rearrange("b a -> a b"), y_row[:, :]).then_inc(y_out, 16)
            act.wait_ge(y_out, 16)

        @block.vector
        def _(dve):
            for name, s in (("scaled", scaled), ("var_ready", var_ready), ("z_read", z_read),
                            ("regrouped_dve", regrouped_dve)):
                dve.sem_inc(s, C[name])
            dve.memset(ones[:, :], 1.0)
            dve.memset(eps[:, :], EPS)
            dve.memset(ws_block[:, :], 0.0).then_inc(consts_set, 1)
            dve.wait_ge(weights_in, 16 * 11)

            def centre(dst, src, mean, width, step):
                dve.tensor_reduce(mean, src, AX_X, ALU.add).then_inc(centred, 1)
                dve.wait_ge(centred, step)
                dve.tensor_scalar(mean, mean, 1.0 / width, None, ALU.mult).then_inc(centred, 1)
                dve.wait_ge(centred, step + 1)
                return dve.tensor_tensor(dst, src, mean.to_broadcast(list(src.shape)) if mean.ndim == src.ndim
                                         else mean.unsqueeze(mean.ndim).to_broadcast(list(src.shape)), ALU.subtract)

            dve.wait_ge(consts_set, 1)
            centre(ws2[:, :], ws2[:, :], means[:, 0:1], E, 1).then_inc(centred, 1)
            dve.wait_ge(centred, 3)
            for s in range(2):
                last = dve.tensor_copy(ws_block[D * s:D * (s + 1), E * s:E * (s + 1)], ws2[D * s:D * (s + 1), :])
            last.then_inc(consts_set, 1)
            centre(wd[:, :, :], wd[:, :, :], means[:, 2:2 + FC], E, 4).then_inc(consts_set, 1)
            centre(wsi4[:, :], wsi4[:, :], means[0:QN, 1:2], PR, 6).then_inc(centred, 1)
            dve.wait_ge(centred, 8)
            for q in range(Q):
                dve.tensor_copy(wsi_c[:, q, :], wsi4[:, :])
                last = dve.tensor_scalar(wsi_block[0:QN, PR * q:PR * (q + 1)], wsi4[:, :], mask[:, q:q + 1], None, ALU.mult)
            last.then_inc(consts_set, 1)

            def recip_proj(t, j, c):
                s, w = (j + c) % 2, 2 * pairs_in(c, PP)
                dve.wait_ge(proj_std, PCH * t + c + 1)
                dve.reciprocal(proj_rs[s][:, 0:w], proj_sd[s][:, 0:w]).then_inc(proj_rstd, 1)

            def scale_proj(t, j, k, c):
                s = (j + c) % 2
                if c == 0:
                    dve.wait_ge(stored[j % 2], 16 * (k + 1))
                dve.wait_ge(proj_rstd, PCH * t + c + 1)
                for a in range(2 * pairs_in(c, PP)):
                    last = dve.scalar_tensor_tensor(
                        out=normed[j % 2][:, 2 * PP * c + a, :], in0=proj_ps[s][:, E * a:E * (a + 1)],
                        scalar=proj_rs[s][:, a:a + 1], in1=gs_b[:, :], op0=ALU.mult, op1=ALU.mult)
                last.then_inc(scaled, 1)

            def reduce_z(t, m):
                dve.wait_ge(squared, UN * t + m + 1)
                dve.tensor_reduce(z_var[m % 2][:, :], z_sq[m % 2][:, :, :], AX_X, ALU.add).then_inc(var_ready, 1)

            def finish_items(t, m):
                s = m % 2
                dve.wait_ge(z_std, UN * t + m + 1)
                dve.reciprocal(z_rs[s][:, :], z_sd[s][:, :]).then_inc(z_rstd, 1)
                dve.wait_ge(paired, UN * t + m + 1)
                dve.tensor_copy(items[m % 4][:, :, 0], x_all[:, bass.ds(P * t + UR * m, UR)])
                dve.wait_ge(z_rstd, UN * t + m + 1)
                dve.tensor_tensor(z_n[s][:, :, :], z_ps[s][:, :, :],
                                  z_rs[s][:, :].unsqueeze(2).to_broadcast([P, UR, PR]), ALU.mult).then_inc(z_read, 1)
                dve.wait_ge(z_read, C["z_read"] + UN * t + m + 1)
                dve.tensor_tensor(z_n[s][:, :, :], z_n[s][:, :, :],
                                  gsi_b[:, :].unsqueeze(1).to_broadcast([P, UR, PR]), ALU.mult).then_inc(z_scaled, 1)
                dve.wait_ge(z_scaled, UN * t + m + 1)
                dve.tensor_tensor(items[m % 4][:, :, 1:PR + 1], z_n[s][:, :, :],
                                  bsi_b[:, :].unsqueeze(1).to_broadcast([P, UR, PR]), ALU.add).then_inc(items_ready, 1)

            def regroup(t, j, h):
                dve.wait_ge(paired, C["paired"] + UN * t + UN // 2 * (h + 1))
                for q in range(Q):
                    for jg in range(Q):
                        last = dve.tensor_copy(*regroup_block(j, h, q, jg))
                last.then_inc(regrouped_dve, 1)

            def ahead(t, j):
                for kind, c in AHEAD:
                    if kind == "p":
                        recip_proj(t, j, c)
                        scale_proj(t, j, 0, c)

            ahead(0, 0)
            ahead(1, 1)
            for blk in range(SUPER):
                xs = x_all[:, SB * blk:SB * (blk + 1)]
                dve.wait_ge(prep_read, 2 * blk + 3)
                dve.reciprocal(wide_rs[:, :], wide_sd[:, :]).then_inc(x_scaled, 1)
                dve.wait_ge(x_scaled, 4 * blk + 1)
                dve.tensor_tensor(xs, pair_c[:, 0, :], wide_rs[:, :], ALU.mult).then_inc(x_scaled, 1)
                dve.wait_ge(x_scaled, 4 * blk + 2)
                dve.tensor_scalar(xs, xs, col["gd"][0], col["bd"][0], ALU.mult, ALU.add).then_inc(x_scaled, 2)
            dve.wait_ge(late_in, 64)
            centre(wl[:, :, :], wl[:, :, :], means[:, 2 + FC:2 + FC + JJ], O, 9).then_inc(consts_set, 2)
            dve.wait_ge(x_scaled, 4 * SUPER)

            def tile(i, j, more):
                t, k = JT * i + j, 2 * i + j // 2
                for kind, c in ORDER:
                    if kind == "z":
                        reduce_z(t, c)
                        if c >= 1:
                            finish_items(t, c - 1)
                        if c == UN - 1:
                            finish_items(t, c)
                    elif kind == "g":
                        if c == UN - 1:
                            regroup(t, j, 1)
                    elif more and kind == "p":
                        recip_proj(t + 2, j, c)
                        scale_proj(t + 2, j, k + 1, c)

            def top(i):
                step = 3 * i
                dve.wait_ge(top_read, C["top_read"] + TOPS * i + OC + 1)
                dve.reciprocal(wide_rs[:, :], wide_sd[:, :]).then_inc(hidden0_step, 1)
                dve.wait_ge(hidden0_step, step + 1)
                dve.tensor_tensor(hidden0[:, :, :], pair_c[:, 0:ZC, :],
                                  wide_rs[:, :].unsqueeze(1).to_broadcast([P, ZC, SB]), ALU.mult).then_inc(hidden0_step, 1)
                dve.wait_ge(hidden0_step, step + 2)
                for c in range(ZC):
                    last = dve.tensor_scalar(hidden0[:, c, :], hidden0[:, c, :], col["gl"][c], col["bl"][c],
                                             ALU.mult, ALU.add)
                last.then_inc(hidden0_step, 1)

            with dve.Fori(0, SUPER - 1) as i:
                for j in range(JT):
                    tile(i, j, True)
                top(i)
            for j in range(JT):
                tile(SUPER - 1, j, j < 2)
            top(SUPER - 1)


def kernel(**inputs):
    import numpy as np
    import concourse.bacc as bacc
    from concourse.bass_utils import run_bass_kernel_spmd

    a = {k: np.ascontiguousarray(v) for k, v in inputs.items()}
    N, D = 26, 64
    E = a["L0_rec_Wd"].shape[0]
    PR = a["L0_rec_Wsi"].shape[0]
    O = a["L0_rec_Wl"].shape[0]
    Q, JJ = 128 // PR, PR // (128 // PR)

    def columns(v):
        return v.reshape(-1, 128).T

    wl = np.zeros((Q, PR, JJ, O), np.float32)
    wl_t = a["L0_rec_Wl"].T
    for p in range(PR):
        for j in range(p + 1):
            wl[j // JJ, p, j % JJ] = wl_t[p * (p + 1) // 2 + j]
    arrays = {"ids": a["ids"]}
    for n in range(N):
        arrays[f"tbl_{n}"] = a[f"tbl_{n}"]
    arrays.update(
        dense_t=a["r_dense_t"].T,
        ident=np.eye(128, dtype=np.float32),
        wd_t=a["L0_rec_Wd"].T,
        ws_t2=np.concatenate([a["L0_rec_Ws"].T] * 2, axis=0),
        wsi_t4=np.concatenate([a["L0_rec_Wsi"].T] * Q, axis=0),
        block_mask=np.repeat(np.eye(Q, dtype=np.float32), N, axis=0),
        first_block=np.repeat(np.eye(Q, dtype=np.float32)[:, 0:1], N, axis=0),
        bs_row=np.tile(a["L0_rec_bs"], (128 // Q, 1)),
        gs_rows=np.tile(a["L0_rec_gs"], (128, 1)),
        gsi_rows=np.tile(a["L0_rec_gsi"], (128, 1)),
        bsi_rows=np.tile(a["L0_rec_bsi"], (128, 1)),
        columns=np.concatenate([columns(a[k]) for k in ("L0_rec_gd", "L0_rec_bd", "L0_rec_gl", "L0_rec_bl",
                                                        "b_top1", "b_top2")] + [columns(a["W_top3"][:, 0])], axis=1),
        wl_pairs=wl.reshape(128, JJ, O),
        w_top1=a["W_top1"],
        w_top2=a["W_top2"],
    )
    arrays = {f"in_{k}": np.ascontiguousarray(v) for k, v in arrays.items()}
    nc = bacc.Bacc("TRN2", target_bir_lowering=False, num_devices=1)
    aps = [nc.dram_tensor(k, v.shape, mybir.dt.from_np(v.dtype), kind="ExternalInput").ap() for k, v in arrays.items()]
    out = nc.dram_tensor("out_y", (a["ids"].shape[0], 1), mybir.dt.float32, kind="ExternalOutput").ap()
    dlrm_tower(nc, aps[0], aps[1:1 + N], *aps[1 + N:], out)
    r = run_bass_kernel_spmd(nc, [arrays], core_ids=[0])
    return r.results[0]["out_y"]
```

```python
from contextlib import ExitStack

import concourse.bass as bass
from concourse import mybir

P = 128
ALU = mybir.AluOpType
ACT = mybir.ActivationFunctionType
F32 = mybir.dt.float32
AX_X = mybir.AxisListType.X
EPS = 1e-5

CREDIT = {
    "transposed": 8, "emb_t_ready": 1, "projected": 7, "scaled": 2, "compressed": 16, "var_ready": 2,
    "z_read": 2, "paired": 4, "regrouped": 2, "top_read": 1,
}

PE_ORDER = ("z0 t0 z1 p0 O0 g0 z2 p1 O1 g1 z3 t1 O2 g2 z4 p2 O3 g3 z5 p3 t2 V0 g4 z6 p4 A0 g5 z7 A1 A2 A3 "
            "p5 t3 g6 B0 p6 B1 g7 Y0").split()
ACT_ORDER = ("z0 t0 v0 z1 p0 v1 z2 p1 v2 z3 t1 v3 z4 p2 v4 O3 z5 r0 p3 v5 t2 V0 z6 p4 v6 z7 v7 A3 "
             "p5 t3 p6 B1 Y0 r1").split()
DVE_ORDER = ("z0 f0 z1 p0 f1 z2 p1 f2 z3 f3 z4 p2 f4 z5 p3 f5 V0 z6 p4 f6 z7 f7 p5 p6").split()


def dlrm_tower(nc: bass.Bass, ids, tables, dense_t, ident, wd_t, ws_t2, wsi_t4, block_mask, first_block, bs_row,
               gs_rows, gsi_rows, bsi_rows, columns, wl_pairs, w_top1, w_top2, out):
    B, N = ids.shape
    D = tables[0].shape[1]
    E = wd_t.shape[1]
    FD = dense_t.shape[0]
    PR = wsi_t4.shape[1]
    JJ, O = wl_pairs.shape[1:]
    H1, H2 = w_top1.shape[1], w_top2.shape[1]
    FC = FD // P
    Q = P // PR
    QN = Q * N
    G = P // Q
    TILES = B // P
    XB = 512
    XBLK = B // XB
    UN = 8
    GU = G // UN
    UR = Q * GU
    NPAIR = N // 2
    TP = 4
    TCH = -(-NPAIR // TP)
    PP = 2
    PCH = -(-NPAIR // PP)
    OC = O // P
    ZC = 3
    H1C, H2C = H1 // P, H2 // P
    TOPS = 5
    assert (B, N, D, E, PR, O) == (2048, 26, 64, 128, 32, 512) and JJ * Q == PR

    scratch = [nc.dram_tensor(f"normed_dram{s}", (P * N, E), F32, kind="Internal").ap() for s in range(2)]

    with ExitStack() as ctx:
        def sb(name, shape, dt=F32):
            return ctx.enter_context(nc.sbuf_tensor(name, shape, dt))

        def psum(name, shape):
            return ctx.enter_context(nc.psum_tensor(name, shape, F32))

        def sem(name):
            return ctx.enter_context(nc.semaphore(name))

        ident_sb = sb("ident_sb", [P, P])
        ones = sb("ones", [P, P])
        eps = sb("eps", [P, 1])
        wd = sb("wd", [P, FC, E])
        ws2 = sb("ws2", [P, E])
        ws_block = sb("ws_block", [P, 2 * E])
        wsi4 = sb("wsi4", [QN, PR])
        wsi_c = sb("wsi_c", [QN, Q, PR])
        mask = sb("mask", [QN, Q])
        first = sb("first", [QN, 1])
        wsi_block = sb("wsi_block", [QN + 1, P])
        sum_row = sb("sum_row", [1, P])
        gs_b = sb("gs_b", [P, E])
        gsi_b = sb("gsi_b", [P, PR])
        bsi_b = sb("bsi_b", [P, PR])
        cols = sb("cols", [P, columns.shape[1]])
        wl = sb("wl", [P, JJ, O])
        w1 = sb("w1", [P, ZC + FC, H1])
        w2 = sb("w2", [P, H1C, H2])
        dense = sb("dense", [P, FC, B])
        x_all = sb("x_all", [P, B])
        means = sb("means", [P, FC + 2 + JJ])
        at = 0
        col = {}
        for name, k in (("gd", 1), ("bd", 1), ("gl", OC), ("bl", OC), ("b1", H1C), ("b2", H2C), ("w3", H2C)):
            col[name] = [cols[:, at + c:at + c + 1] for c in range(k)]
            at += k

        idx = [sb(f"idx{s}", [P, N], ids.dtype) for s in range(2)]
        emb = [sb(f"emb{s}", [P, N * D]) for s in range(2)]
        emb_t = [sb(f"emb_t{s}", [P, TP * P]) for s in range(2)]
        junk = [sb(f"junk{s}", [P, 2 * PP, E]) for s in range(2)]
        proj_ss = [sb(f"proj_ss{s}", [P, 2 * PP]) for s in range(2)]
        proj_sd = [sb(f"proj_sd{s}", [P, 2 * PP]) for s in range(2)]
        proj_rs = [sb(f"proj_rs{s}", [P, 2 * PP]) for s in range(2)]
        normed = [sb(f"normed{s}", [P, N, E]) for s in range(2)]
        by_group = [sb(f"by_group{s}", [QN + 1, G, E]) for s in range(2)]
        z_sq = [sb(f"z_sq{s}", [P, UR, PR]) for s in range(2)]
        z_var = [sb(f"z_var{s}", [P, UR]) for s in range(2)]
        z_sd = [sb(f"z_sd{s}", [P, UR]) for s in range(2)]
        z_rs = [sb(f"z_rs{s}", [P, UR]) for s in range(2)]
        z_n = [sb(f"z_n{s}", [P, UR, PR]) for s in range(2)]
        items = [sb(f"items{s}", [P, UR, PR + 1]) for s in range(4)]
        pairs = [sb(f"pairs{s}", [P, JJ, P]) for s in range(2)]
        pair_c = sb("pair_c", [P, OC, P])
        pair_sq = sb("pair_sq", [P, OC, P])
        pair_sd = sb("pair_sd", [P, P])
        pair_rs = sb("pair_rs", [P, P])
        hidden0 = sb("hidden0", [P, ZC, P])
        hidden1 = sb("hidden1", [P, H1C, P])
        hidden2 = sb("hidden2", [P, H2C, P])
        x_raw = sb("x_raw", [P, XB])
        x_sq = sb("x_sq", [P, XB])
        x_sd = sb("x_sd", [P, XB])
        x_rs = sb("x_rs", [P, XB])
        y_row = sb("y_row", [1, B])

        emb_t_ps = psum("emb_t_ps", [P, TP * P])
        proj_ps = [psum(f"proj_ps{s}", [P, 2 * PP * E]) for s in range(2)]
        z_ps = [psum(f"z_ps{s}", [P, UR, PR]) for s in range(2)]
        gram_ps = [psum(f"gram_ps{s}", [P, G // 2, PR]) for s in range(2)]
        top_ps = psum("top_ps", [P, OC, P])
        top_flat = top_ps[:, :, :].rearrange("p a b -> p (a b)")

        weights_in = sem("weights_in")
        late_in = sem("late_in")
        bias_row_in = sem("bias_row_in")
        consts_set = sem("consts_set")
        prep_done = sem("prep_done")
        prep_read = sem("prep_read")
        centred = sem("centred")
        x_scaled = sem("x_scaled")
        ids_in = [sem(f"ids_in{s}") for s in range(2)]
        gathered = [sem(f"gathered{s}") for s in range(2)]
        stored = [sem(f"stored{s}") for s in range(2)]
        loaded = [sem(f"loaded{s}") for s in range(2)]
        transposed = sem("transposed")
        emb_t_ready = sem("emb_t_ready")
        projected = sem("projected")
        proj_sq = sem("proj_sq")
        proj_std = sem("proj_std")
        proj_rstd = sem("proj_rstd")
        scaled = sem("scaled")
        compressed = sem("compressed")
        squared = sem("squared")
        var_ready = sem("var_ready")
        z_std = sem("z_std")
        z_rstd = sem("z_rstd")
        z_read = sem("z_read")
        z_scaled = sem("z_scaled")
        items_ready = sem("items_ready")
        paired = sem("paired")
        regrouped = sem("regrouped")
        top_done = sem("top_done")
        top_read = sem("top_read")
        hidden0_step = sem("hidden0_step")
        pool_turn = sem("pool_turn")
        y_out = sem("y_out")

        C = CREDIT
        block = ctx.enter_context(nc.Block())

        @block.sync
        def _(sp):
            ids_v = ids.rearrange("(t p) n -> t p n", p=P)

            def load_ids(t, s):
                sp.dma_start(idx[s][:, :], ids_v[bass.ds(t, 1), :, :].rearrange("a p n -> (a p) n")).then_inc(ids_in[s], 16)

            load_ids(0, 0)
            load_ids(1, 1)
            for s in range(2):
                sp.sem_inc(stored[s], 16)
            sp.dma_start(ws2[:, :], ws_t2).then_inc(weights_in, 16)
            sp.dma_start(ident_sb[:, :], ident).then_inc(weights_in, 16)
            sp.dma_start(wd[:, :, :], wd_t.rearrange("(c p) e -> p c e", p=P)).then_inc(weights_in, 16)
            sp.dma_start(wsi4[:, :], wsi_t4).then_inc(weights_in, 16)
            sp.dma_start(mask[:, :], block_mask).then_inc(weights_in, 16)
            sp.dma_start(first[:, :], first_block).then_inc(weights_in, 16)
            sp.dma_start(gs_b[:, :], gs_rows).then_inc(weights_in, 16)
            sp.dma_start(gsi_b[:, :], gsi_rows).then_inc(weights_in, 16)
            sp.dma_start(bsi_b[:, :], bsi_rows).then_inc(weights_in, 16)
            sp.dma_start(cols[:, :], columns).then_inc(weights_in, 16)
            sp.dma_start(dense[:, :, :], dense_t.rearrange("(c p) b -> p c b", p=P)).then_inc(weights_in, 16)
            for s in range(2):
                sp.dma_start(by_group[s][QN:QN + 1, :, :], bs_row.rearrange("(a g) e -> a g e", a=1)).then_inc(bias_row_in, 16)
            sp.dma_start(wl[:, :, :], wl_pairs).then_inc(late_in, 16)
            sp.dma_start(w1[:, 0:ZC, :], w_top1[0:ZC * P, :].rearrange("(c p) h -> p c h", p=P)).then_inc(late_in, 16)
            sp.dma_start(w1[:, ZC:ZC + FC, :], w_top1[O:O + FD, :].rearrange("(c p) h -> p c h", p=P)).then_inc(late_in, 16)
            sp.dma_start(w2[:, :, :], w_top2.rearrange("(c p) h -> p c h", p=P)).then_inc(late_in, 16)
            sp.wait_ge(prep_read, 1)
            sp.dma_start(wsi_block[QN:QN + 1, :], sum_row[0:1, :]).then_inc(bias_row_in, 16)

            def tile(i, s, more):
                t = 2 * i + s
                if more:
                    sp.wait_ge(gathered[s], 16 * N * (i + 1))
                    load_ids(t + 2, s)
                sp.wait_ge(scaled, C["scaled"] + PCH * (t + 1))
                sp.dma_start(scratch[s].rearrange("(p n) e -> p (n e)", n=N),
                             normed[s][:, :, :].rearrange("p n e -> p (n e)")).then_inc(stored[s], 16)
                sp.wait_ge(stored[s], 16 * (i + 2))
                sp.wait_ge(compressed, C["compressed"] + UN * (t - 1))
                sp.dma_start(by_group[s][0:QN, :, :],
                             scratch[s].rearrange("(g r) e -> r g e", r=QN)).then_inc(loaded[s], 16)

            with sp.Fori(0, TILES // 2 - 1) as i:
                tile(i, 0, True)
                tile(i, 1, True)
            tile(TILES // 2 - 1, 0, False)
            tile(TILES // 2 - 1, 1, False)

        @block.gpsimd
        def _(pool):
            with pool.Fori(0, TILES // 2) as i:
                for s in range(2):
                    t = 2 * i + s
                    pool.wait_ge(ids_in[s], 16 * (i + 1))
                    pool.wait_ge(transposed, C["transposed"] + TCH * (t - 1))
                    pool.sem_inc(pool_turn, 1)
                    for n in range(N):
                        pool.indirect_dma_start(
                            emb[s][:, D * n:D * (n + 1)], None, tables[n][:, :],
                            bass.IndirectOffsetOnAxis(ap=idx[s][:, n:n + 1], axis=0)).then_inc(gathered[s], 16)

        def pairs_in(chunk, size):
            return min(size, NPAIR - chunk * size)

        def regroup_block(s, h, q, jg):
            dst = pairs[s][PR * jg:PR * (jg + 1), :, P // 2 * h + q:P // 2 * (h + 1):Q]
            src = gram_ps[h][PR * q:PR * (q + 1), :, JJ * jg:JJ * (jg + 1)].rearrange("p g j -> p j g")
            return dst, src

        @block.tensor
        def _(pe):
            for name, s in (("transposed", transposed), ("projected", projected), ("compressed", compressed),
                            ("paired", paired)):
                pe.sem_inc(s, C[name])

            def transpose(t, s, c):
                if c == 0:
                    pe.wait_ge(gathered[s], 8 * N * (t - s) + 16 * N)
                pe.wait_ge(emb_t_ready, C["emb_t_ready"] + TCH * t + c)
                for a in range(pairs_in(c, TP)):
                    at = 2 * D * (TP * c + a)
                    last = pe.transpose(emb_t_ps[:, P * a:P * (a + 1)], emb[s][:, at:at + 2 * D], ident_sb[:, :])
                last.then_inc(transposed, 1)

            def project(t, s, c):
                if c % 2 == 0:
                    pe.wait_ge(emb_t_ready, C["emb_t_ready"] + TCH * t + c // 2 + 1)
                pe.wait_ge(scaled, PCH * t + c + 1)
                for a in range(pairs_in(c, PP)):
                    at = P * (PP * (c % 2) + a)
                    last = pe.matmul(proj_ps[(s + c) % 2][:, 2 * E * a:2 * E * (a + 1)], emb_t[c // 2 % 2][:, at:at + P],
                                     ws_block[:, :], start=True, stop=True)
                last.then_inc(projected, 1)

            def compress(t, s, m):
                if m == 0:
                    pe.wait_ge(loaded[s], 8 * (t - s) + 16)
                pe.wait_ge(z_read, UN * t + m + 1)
                for a in range(GU):
                    last = pe.matmul(z_ps[m % 2][:, Q * a:Q * (a + 1), :], by_group[s][:, GU * m + a, :],
                                     wsi_block[:, :], start=True, stop=True)
                last.then_inc(compressed, 1)

            def pair(t, m):
                h = m // (UN // 2)
                if m % (UN // 2) == 0:
                    pe.wait_ge(regrouped, 2 * t + h + 1)
                pe.wait_ge(items_ready, UN * t + m + 1)
                it = items[m % 4]
                for a in range(GU):
                    g = GU * (m % (UN // 2)) + a
                    for q in range(Q):
                        r = Q * a + q
                        last = pe.matmul(gram_ps[h][PR * q:PR * (q + 1), g, :], it[:, r, 1:PR + 1], it[:, r, 0:PR],
                                         start=True, stop=True)
                last.then_inc(paired, 1)

            def top(t, s, kind, c):
                if kind == "O":
                    if c == 0:
                        pe.wait_ge(top_read, C["top_read"] + TOPS * t)
                        pe.wait_ge(regrouped, C["regrouped"] + 2 * t + 2)
                    for jj in range(JJ):
                        last = pe.matmul(top_ps[:, c, :], wl[:, jj, P * c:P * (c + 1)], pairs[s][:, jj, :],
                                         start=jj == 0, stop=jj == JJ - 1)
                    if c == OC - 1:
                        last.then_inc(top_done, 1)
                elif kind == "V":
                    pe.wait_ge(top_read, C["top_read"] + TOPS * t + 1)
                    for oc in range(OC):
                        last = pe.matmul(top_ps[:, 0, :], ones[:, :], pair_sq[:, oc, :], start=oc == 0, stop=oc == OC - 1)
                    last.then_inc(top_done, 1)
                elif kind == "A":
                    if c == 0:
                        pe.wait_ge(top_read, C["top_read"] + TOPS * t + 2)
                    for f in range(FC):
                        pe.matmul(top_ps[:, c, :], w1[:, ZC + f, P * c:P * (c + 1)], dense[:, f, bass.ds(P * t, P)],
                                  start=f == 0, stop=False)
                    for o in range(ZC):
                        if c == 0 and o == 0:
                            pe.wait_ge(hidden0_step, 3 * t + 3)
                        last = pe.matmul(top_ps[:, c, :], w1[:, o, P * c:P * (c + 1)], hidden0[:, o, :],
                                         start=False, stop=o == ZC - 1)
                    if c == H1C - 1:
                        last.then_inc(top_done, 1)
                elif kind == "B":
                    if c == 0:
                        pe.wait_ge(top_read, C["top_read"] + TOPS * t + 3)
                    for h in range(H1C):
                        last = pe.matmul(top_ps[:, c, :], w2[:, h, P * c:P * (c + 1)], hidden1[:, h, :],
                                         start=h == 0, stop=h == H1C - 1)
                    if c == H2C - 1:
                        last.then_inc(top_done, 1)
                else:
                    pe.wait_ge(top_read, C["top_read"] + TOPS * t + 4)
                    for h in range(H2C):
                        last = pe.matmul(top_ps[0:1, 0, :], col["w3"][h], hidden2[:, h, :], start=h == 0, stop=h == H2C - 1)
                    last.then_inc(top_done, 1)

            pe.wait_ge(consts_set, 4)
            pe.matmul(top_flat[0:1, 0:P], first[:, :], wsi_c[:, :, :].rearrange("r q p -> r (q p)"),
                      start=True, stop=True).then_inc(prep_done, 1)
            for blk in range(XBLK):
                pe.wait_ge(prep_read, 2 * blk + 1)
                for c in range(FC):
                    last = pe.matmul(top_flat, wd[:, c, :], dense[:, c, XB * blk:XB * (blk + 1)],
                                     start=c == 0, stop=c == FC - 1)
                last.then_inc(prep_done, 1)
                pe.wait_ge(prep_read, 2 * blk + 2)
                pe.matmul(top_flat, ones[:, :], x_sq[:, :], start=True, stop=True).then_inc(prep_done, 1)

            def step(i, s, ahead=True, behind=True):
                t = 2 * i + s
                for item in PE_ORDER:
                    kind, c = item[0], int(item[1:])
                    if kind == "z":
                        compress(t, s, c)
                    elif kind == "g":
                        pair(t, c)
                    elif kind == "t":
                        if ahead:
                            transpose(t + 2, s, c)
                    elif kind == "p":
                        if ahead:
                            project(t + 2, s, c)
                    elif behind:
                        top(t - 1, 1 - s, kind, c)

            for t in range(2):
                for item in PE_ORDER:
                    if item[0] in "tp":
                        (transpose if item[0] == "t" else project)(t, t, int(item[1:]))
            pe.wait_ge(bias_row_in, 48)
            pe.wait_ge(prep_read, 2 * XBLK + 1)
            pe.wait_ge(late_in, 64)
            pe.wait_ge(consts_set, 6)
            step(0, 0, behind=False)
            step(0, 1)
            with pe.Fori(1, TILES // 2 - 1) as i:
                step(i, 0)
                step(i, 1)
            step(TILES // 2 - 1, 0, ahead=False)
            step(TILES // 2 - 1, 1, ahead=False)
            for item in PE_ORDER:
                if item[0] in "OVABY":
                    top(TILES - 1, 1, item[0], int(item[1:]))

        @block.scalar
        def _(act):
            for name, s in (("emb_t_ready", emb_t_ready), ("regrouped", regrouped), ("top_read", top_read)):
                act.sem_inc(s, C[name])

            def copy_emb_t(t, c):
                act.wait_ge(transposed, C["transposed"] + TCH * t + c + 1)
                before = PCH * t + (2 * c - 2 if c >= 2 else c - 1)
                act.wait_ge(projected, C["projected"] + before)
                w = P * pairs_in(c, TP)
                act.activation(emb_t[c % 2][:, 0:w], emb_t_ps[:, 0:w], ACT.Copy).then_inc(emb_t_ready, 1)

            def square_proj(t, j, c):
                act.wait_ge(projected, C["projected"] + PCH * t + c + 1)
                s = (j + c) % 2
                for a in range(2 * pairs_in(c, PP)):
                    last = act.activation(junk[s][:, a, :], proj_ps[s][:, E * a:E * (a + 1)], ACT.Square,
                                          accum_out=proj_ss[s][:, a:a + 1])
                last.then_inc(proj_sq, 1)

            def std_proj(t, j, c):
                s, w = (j + c) % 2, 2 * pairs_in(c, PP)
                act.wait_ge(proj_sq, PCH * t + c + 1)
                act.activation(proj_sd[s][:, 0:w], proj_ss[s][:, 0:w], ACT.Sqrt, bias=eps[:, :],
                               scale=1.0 / E).then_inc(proj_std, 1)

            def square_z(t, m):
                act.wait_ge(compressed, C["compressed"] + UN * t + m + 1)
                act.wait_ge(var_ready, UN * t + m + 1)
                act.activation(z_sq[m % 2][:, :, :], z_ps[m % 2][:, :, :], ACT.Square).then_inc(squared, 1)

            def std_z(t, m):
                act.wait_ge(var_ready, C["var_ready"] + UN * t + m + 1)
                act.activation(z_sd[m % 2][:, :], z_var[m % 2][:, :], ACT.Sqrt, bias=eps[:, :],
                               scale=1.0 / PR).then_inc(z_std, 1)

            def regroup(t, s, h):
                act.wait_ge(paired, C["paired"] + UN * t + UN // 2 * (h + 1))
                for q in range(Q):
                    for jg in range(Q):
                        last = act.activation(*regroup_block(s, h, q, jg), ACT.Copy)
                last.then_inc(regrouped, 1)

            def top(t, kind):
                def done(k):
                    act.wait_ge(top_done, TOPS * t + k)

                if kind == "O":
                    done(1)
                    act.activation(pair_c[:, :, :], top_ps[:, :, :], ACT.Copy)
                    act.activation(pair_sq[:, :, :], top_ps[:, :, :], ACT.Square).then_inc(top_read, 1)
                elif kind == "V":
                    done(2)
                    act.activation(pair_sd[:, :], top_ps[:, 0, :], ACT.Sqrt, bias=eps[:, :],
                                   scale=1.0 / O).then_inc(top_read, 1)
                elif kind == "A":
                    done(3)
                    for h in range(H1C):
                        last = act.activation(hidden1[:, h, :], top_ps[:, h, :], ACT.Relu, bias=col["b1"][h])
                    last.then_inc(top_read, 1)
                elif kind == "B":
                    done(4)
                    for h in range(H2C):
                        last = act.activation(hidden2[:, h, :], top_ps[:, h, :], ACT.Relu, bias=col["b2"][h])
                    last.then_inc(top_read, 1)
                else:
                    done(5)
                    act.activation(y_row[0:1, bass.ds(P * t, P)], top_ps[0:1, 0, :], ACT.Copy).then_inc(top_read, 1)

            act.wait_ge(consts_set, 3)
            act.wait_ge(prep_done, 1)
            act.activation(sum_row[:, :], top_flat[0:1, 0:P], ACT.Copy).then_inc(prep_read, 1)
            for blk in range(XBLK):
                act.wait_ge(prep_done, 2 * blk + 2)
                if blk >= 1:
                    act.wait_ge(x_scaled, 4 * blk)
                act.activation(x_raw[:, :], top_flat, ACT.Copy)
                act.activation(x_sq[:, :], top_flat, ACT.Square).then_inc(prep_read, 1)
                act.wait_ge(prep_done, 2 * blk + 3)
                act.activation(x_sd[:, :], top_flat, ACT.Sqrt, bias=eps[:, :], scale=1.0 / E).then_inc(prep_read, 1)

            def step(i, s, ahead=True, behind=True):
                t = 2 * i + s
                for item in ACT_ORDER:
                    kind, c = item[0], int(item[1:])
                    if kind == "z":
                        square_z(t, c)
                    elif kind == "v":
                        std_z(t, c)
                    elif kind == "r":
                        regroup(t, s, c)
                    elif kind == "t":
                        if ahead:
                            copy_emb_t(t + 2, c)
                    elif kind == "p":
                        if ahead:
                            square_proj(t + 2, s, c)
                            std_proj(t + 2, s, c)
                    elif behind:
                        top(t - 1, kind)

            for t in range(2):
                for item in ACT_ORDER:
                    if item[0] == "t":
                        copy_emb_t(t, int(item[1:]))
                    elif item[0] == "p":
                        square_proj(t, t, int(item[1:]))
                        std_proj(t, t, int(item[1:]))
            step(0, 0, behind=False)
            step(0, 1)
            with act.Fori(1, TILES // 2 - 1) as i:
                step(i, 0)
                step(i, 1)
            step(TILES // 2 - 1, 0, ahead=False)
            step(TILES // 2 - 1, 1, ahead=False)
            for kind in "OVABY":
                top(TILES - 1, kind)
            act.wait_ge(top_read, C["top_read"] + TOPS * TILES)
            act.dma_start(out.rearrange("b a -> a b"), y_row[:, :]).then_inc(y_out, 16)
            act.wait_ge(y_out, 16)

        @block.vector
        def _(dve):
            for name, s in (("scaled", scaled), ("var_ready", var_ready), ("z_read", z_read)):
                dve.sem_inc(s, C[name])
            dve.memset(ones[:, :], 1.0)
            dve.memset(eps[:, :], EPS)
            dve.memset(ws_block[:, :], 0.0).then_inc(consts_set, 1)
            dve.wait_ge(weights_in, 16 * 11)

            def centre(dst, src, mean, width, step):
                dve.tensor_reduce(mean, src, AX_X, ALU.add).then_inc(centred, 1)
                dve.wait_ge(centred, step)
                dve.tensor_scalar(mean, mean, 1.0 / width, None, ALU.mult).then_inc(centred, 1)
                dve.wait_ge(centred, step + 1)
                return dve.tensor_tensor(dst, src, mean.to_broadcast(list(src.shape)) if mean.ndim == src.ndim
                                         else mean.unsqueeze(mean.ndim).to_broadcast(list(src.shape)), ALU.subtract)

            dve.wait_ge(consts_set, 1)
            centre(ws2[:, :], ws2[:, :], means[:, 0:1], E, 1).then_inc(centred, 1)
            dve.wait_ge(centred, 3)
            for s in range(2):
                last = dve.tensor_copy(ws_block[D * s:D * (s + 1), E * s:E * (s + 1)], ws2[D * s:D * (s + 1), :])
            last.then_inc(consts_set, 1)
            centre(wd[:, :, :], wd[:, :, :], means[:, 2:2 + FC], E, 4).then_inc(consts_set, 1)
            centre(wsi4[:, :], wsi4[:, :], means[0:QN, 1:2], PR, 6).then_inc(centred, 1)
            dve.wait_ge(centred, 8)
            for q in range(Q):
                dve.tensor_copy(wsi_c[:, q, :], wsi4[:, :])
                last = dve.tensor_scalar(wsi_block[0:QN, PR * q:PR * (q + 1)], wsi4[:, :], mask[:, q:q + 1], None, ALU.mult)
            last.then_inc(consts_set, 1)

            def recip_proj(t, j, c):
                s, w = (j + c) % 2, 2 * pairs_in(c, PP)
                dve.wait_ge(proj_std, PCH * t + c + 1)
                dve.reciprocal(proj_rs[s][:, 0:w], proj_sd[s][:, 0:w]).then_inc(proj_rstd, 1)

            def scale_proj(t, j, c):
                s = (j + c) % 2
                if c == 0:
                    dve.wait_ge(stored[j], 8 * (t - j) + 16)
                dve.wait_ge(proj_rstd, PCH * t + c + 1)
                for a in range(2 * pairs_in(c, PP)):
                    last = dve.scalar_tensor_tensor(
                        out=normed[j][:, 2 * PP * c + a, :], in0=proj_ps[s][:, E * a:E * (a + 1)],
                        scalar=proj_rs[s][:, a:a + 1], in1=gs_b[:, :], op0=ALU.mult, op1=ALU.mult)
                last.then_inc(scaled, 1)

            def reduce_z(t, m):
                dve.wait_ge(squared, UN * t + m + 1)
                dve.tensor_reduce(z_var[m % 2][:, :], z_sq[m % 2][:, :, :], AX_X, ALU.add).then_inc(var_ready, 1)

            def finish_items(t, m):
                s = m % 2
                dve.wait_ge(z_std, UN * t + m + 1)
                dve.reciprocal(z_rs[s][:, :], z_sd[s][:, :]).then_inc(z_rstd, 1)
                dve.wait_ge(paired, UN * t + m + 1)
                dve.tensor_copy(items[m % 4][:, :, 0], x_all[:, bass.ds(P * t + UR * m, UR)])
                dve.wait_ge(z_rstd, UN * t + m + 1)
                dve.tensor_tensor(z_n[s][:, :, :], z_ps[s][:, :, :],
                                  z_rs[s][:, :].unsqueeze(2).to_broadcast([P, UR, PR]), ALU.mult).then_inc(z_read, 1)
                dve.wait_ge(z_read, C["z_read"] + UN * t + m + 1)
                dve.tensor_tensor(z_n[s][:, :, :], z_n[s][:, :, :],
                                  gsi_b[:, :].unsqueeze(1).to_broadcast([P, UR, PR]), ALU.mult).then_inc(z_scaled, 1)
                dve.wait_ge(z_scaled, UN * t + m + 1)
                dve.tensor_tensor(items[m % 4][:, :, 1:PR + 1], z_n[s][:, :, :],
                                  bsi_b[:, :].unsqueeze(1).to_broadcast([P, UR, PR]), ALU.add).then_inc(items_ready, 1)

            for blk in range(XBLK):
                xs = x_all[:, XB * blk:XB * (blk + 1)]
                dve.wait_ge(prep_read, 2 * blk + 3)
                dve.reciprocal(x_rs[:, :], x_sd[:, :]).then_inc(x_scaled, 1)
                dve.wait_ge(x_scaled, 4 * blk + 1)
                dve.tensor_tensor(xs, x_raw[:, :], x_rs[:, :], ALU.mult).then_inc(x_scaled, 1)
                dve.wait_ge(x_scaled, 4 * blk + 2)
                dve.tensor_scalar(xs, xs, col["gd"][0], col["bd"][0], ALU.mult, ALU.add).then_inc(x_scaled, 2)

            def top_norm(t):
                dve.wait_ge(top_read, C["top_read"] + TOPS * t + 2)
                dve.reciprocal(pair_rs[:, :], pair_sd[:, :]).then_inc(hidden0_step, 1)
                dve.wait_ge(hidden0_step, 3 * t + 1)
                dve.tensor_tensor(hidden0[:, :, :], pair_c[:, 0:ZC, :],
                                  pair_rs[:, :].unsqueeze(1).to_broadcast([P, ZC, P]), ALU.mult).then_inc(hidden0_step, 1)
                dve.wait_ge(hidden0_step, 3 * t + 2)
                for c in range(ZC):
                    last = dve.tensor_scalar(hidden0[:, c, :], hidden0[:, c, :], col["gl"][c], col["bl"][c],
                                             ALU.mult, ALU.add)
                last.then_inc(hidden0_step, 1)

            def step(i, s, ahead=True, behind=True):
                t = 2 * i + s
                for item in DVE_ORDER:
                    kind, c = item[0], int(item[1:])
                    if kind == "z":
                        reduce_z(t, c)
                    elif kind == "f":
                        finish_items(t, c)
                    elif kind == "p":
                        if ahead:
                            recip_proj(t + 2, s, c)
                            scale_proj(t + 2, s, c)
                    elif behind:
                        top_norm(t - 1)

            for t in range(2):
                for c in range(PCH):
                    recip_proj(t, t, c)
                    scale_proj(t, t, c)
                if t == 0:
                    dve.wait_ge(late_in, 64)
                    centre(wl[:, :, :], wl[:, :, :], means[:, 2 + FC:2 + FC + JJ], O, 9).then_inc(consts_set, 2)
            dve.wait_ge(x_scaled, 4 * XBLK)
            step(0, 0, behind=False)
            step(0, 1)
            with dve.Fori(1, TILES // 2 - 1) as i:
                step(i, 0)
                step(i, 1)
            step(TILES // 2 - 1, 0, ahead=False)
            step(TILES // 2 - 1, 1, ahead=False)
            top_norm(TILES - 1)


def kernel(**inputs):
    import numpy as np
    import concourse.bacc as bacc
    from concourse.bass_utils import run_bass_kernel_spmd

    a = {k: np.ascontiguousarray(v) for k, v in inputs.items()}
    N, D = 26, 64
    E = a["L0_rec_Wd"].shape[0]
    PR = a["L0_rec_Wsi"].shape[0]
    O = a["L0_rec_Wl"].shape[0]
    Q, JJ = 128 // PR, PR // (128 // PR)

    def columns(v):
        return v.reshape(-1, 128).T

    wl = np.zeros((Q, PR, JJ, O), np.float32)
    wl_t = a["L0_rec_Wl"].T
    for p in range(PR):
        for j in range(p + 1):
            wl[j // JJ, p, j % JJ] = wl_t[p * (p + 1) // 2 + j]
    arrays = {"ids": a["ids"]}
    for n in range(N):
        arrays[f"tbl_{n}"] = a[f"tbl_{n}"]
    arrays.update(
        dense_t=a["r_dense_t"].T,
        ident=np.eye(128, dtype=np.float32),
        wd_t=a["L0_rec_Wd"].T,
        ws_t2=np.concatenate([a["L0_rec_Ws"].T] * 2, axis=0),
        wsi_t4=np.concatenate([a["L0_rec_Wsi"].T] * Q, axis=0),
        block_mask=np.repeat(np.eye(Q, dtype=np.float32), N, axis=0),
        first_block=np.repeat(np.eye(Q, dtype=np.float32)[:, 0:1], N, axis=0),
        bs_row=np.tile(a["L0_rec_bs"], (128 // Q, 1)),
        gs_rows=np.tile(a["L0_rec_gs"], (128, 1)),
        gsi_rows=np.tile(a["L0_rec_gsi"], (128, 1)),
        bsi_rows=np.tile(a["L0_rec_bsi"], (128, 1)),
        columns=np.concatenate([columns(a[k]) for k in ("L0_rec_gd", "L0_rec_bd", "L0_rec_gl", "L0_rec_bl",
                                                        "b_top1", "b_top2")] + [columns(a["W_top3"][:, 0])], axis=1),
        wl_pairs=wl.reshape(128, JJ, O),
        w_top1=a["W_top1"],
        w_top2=a["W_top2"],
    )
    arrays = {f"in_{k}": np.ascontiguousarray(v) for k, v in arrays.items()}
    nc = bacc.Bacc("TRN2", target_bir_lowering=False, num_devices=1)
    aps = [nc.dram_tensor(k, v.shape, mybir.dt.from_np(v.dtype), kind="ExternalInput").ap() for k, v in arrays.items()]
    out = nc.dram_tensor("out_y", (a["ids"].shape[0], 1), mybir.dt.float32, kind="ExternalOutput").ap()
    dlrm_tower(nc, aps[0], aps[1:1 + N], *aps[1 + N:], out)
    r = run_bass_kernel_spmd(nc, [arrays], core_ids=[0])
    return r.results[0]["out_y"]
```

```python
from contextlib import ExitStack

import concourse.bass as bass
from concourse import mybir

P = 128
ALU = mybir.AluOpType
ACT = mybir.ActivationFunctionType
F32 = mybir.dt.float32
AX_X = mybir.AxisListType.X
EPS = 1e-5

CREDIT = {
    "transposed": 8, "emb_t_ready": 1, "projected": 7, "scaled": 2, "compressed": 16, "var_ready": 2,
    "z_read": 2, "paired": 4, "regrouped": 2, "top_read": 1,
}

ONCE = "XSW"
PE_ORDER = """g4-1 g5-1 p4+1 A0-2 X2+1 A1-2 t3+1 p5+1 z1 A2-2 z2 p6+1 S2+1 A3-2 g6-1 g7-1 g0 X0+2 t0+2 S0+2 B0-2
    B1-2 z3 p0+2 X3+1 p1+2 Y0-2 z4 O0-1 S3+1 O1-1 X1+2 z5 t1+2 O2-1 z6 O3-1 g1 p2+2 z7 V0-1 p3+2 g2 g3 t2+2 D0-1
    z0+1 S1+2""".split()
ACT_ORDER = """z7-1 x5-1 p3+1 t2+1 S1+1 v7-1 H0-2 z0 r0-1 X0+2 v0 p4+1 x6-1 t3+1 z1 x7-1 p5+1 x0 z2 X2+1 S0+2 v1
    p6+1 A3-2 v2 t0+2 r1-1 B1-2 S2+1 z3 Y0-2 p0+2 v3 z4 v4 X3+1 z5 x1 p1+2 v5 S3+1 t1+2 x2 z6 x3 v6 O3-1 x4 p2+2
    V0-1 X1+2""".split()
DVE_ORDER = """M2-1 G1-1 G2-1 z3-1 a1-1 a2-1 W0+2 R3-1 z4-1 X2 M3-1 R4-1 G3-1 M4-1 p0+1 a3-1 z5-1 G4-1 R5-1 a4-1
    M5-1 z6-1 p1+1 G5-1 R6-1 X0+1 a5-1 M6-1 V0-2 X3 p2+1 z7-1 D0-2 p3+1 R7-1 G6-1 M7-1 z0 G7-1 X1+1 a6-1 R0 M0 p4+1
    G0 a7-1 z1 a0 R1 z2 M1 p5+1 p6+1 R2""".split()


def items_of(order, t, tiles):
    for item in order:
        lag = int(item[2:] or 0)
        if item[0] in ONCE:
            runs = isinstance(t, int) and t + lag == 0
        else:
            runs = not isinstance(t, int) or 0 <= t + lag < tiles
        if runs:
            yield item[0], int(item[1]), lag


def dlrm_tower(nc: bass.Bass, ids, tables, dense_t, ident, wd_t, ws_t2, wsi_t4, block_mask, first_block, bs_row,
               gs_rows, gsi_rows, bsi_rows, columns, wl_pairs, w_top1, w_top2, out):
    B, N = ids.shape
    D = tables[0].shape[1]
    E = wd_t.shape[1]
    FD = dense_t.shape[0]
    PR = wsi_t4.shape[1]
    JJ, O = wl_pairs.shape[1:]
    H1, H2 = w_top1.shape[1], w_top2.shape[1]
    FC = FD // P
    Q = P // PR
    QN = Q * N
    G = P // Q
    TILES = B // P
    XB = 512
    XBLK = B // XB
    UN = 8
    GU = G // UN
    UR = Q * GU
    NPAIR = N // 2
    TP = 4
    TCH = -(-NPAIR // TP)
    PP = 2
    PCH = -(-NPAIR // PP)
    N1 = 2 * PP * (PCH // 2 + 1)
    OC = O // P
    ZC = 3
    H1C, H2C = H1 // P, H2 // P
    FIRST_TOP = max(-int(item[2:] or 0) for item in PE_ORDER if item[:2] == "O0")
    assert FIRST_TOP <= 2 and all(int(item[2:] or 0) > -2 for item in PE_ORDER if item[:2] == "z0")
    TOPS = 6
    assert (B, N, D, E, PR, O) == (2048, 26, 64, 128, 32, 512) and JJ * Q == PR

    scratch = [nc.dram_tensor(f"normed_dram{s}", (P * N, E), F32, kind="Internal").ap() for s in range(2)]

    with ExitStack() as ctx:
        def sb(name, shape, dt=F32):
            return ctx.enter_context(nc.sbuf_tensor(name, shape, dt))

        def psum(name, shape):
            return ctx.enter_context(nc.psum_tensor(name, shape, F32))

        def sem(name):
            return ctx.enter_context(nc.semaphore(name))

        ident_sb = sb("ident_sb", [P, P])
        ones = sb("ones", [P, P])
        eps = sb("eps", [P, 1])
        wd = sb("wd", [P, FC, E])
        ws2 = sb("ws2", [P, E])
        ws_block = sb("ws_block", [P, 2 * E])
        wsi4 = sb("wsi4", [QN, PR])
        wsi_c = sb("wsi_c", [QN, Q, PR])
        mask = sb("mask", [QN, Q])
        first = sb("first", [QN, 1])
        wsi_block = sb("wsi_block", [QN + 1, P])
        sum_row = sb("sum_row", [1, P])
        gs_b = sb("gs_b", [P, E])
        gsi_b = sb("gsi_b", [P, PR])
        bsi_b = sb("bsi_b", [P, PR])
        cols = sb("cols", [P, columns.shape[1]])
        wl = sb("wl", [P, JJ, O])
        w1 = sb("w1", [P, ZC + FC, H1])
        w2 = sb("w2", [P, H1C, H2])
        dense = sb("dense", [P, FC, B])
        x_all = sb("x_all", [P, B])
        means = sb("means", [P, FC + 2 + JJ])
        at = 0
        col = {}
        for name, k in (("gd", 1), ("bd", 1), ("gl", OC), ("bl", OC), ("b1", H1C), ("b2", H2C), ("w3", H2C)):
            col[name] = [cols[:, at + c:at + c + 1] for c in range(k)]
            at += k

        idx = [sb(f"idx{s}", [P, N], ids.dtype) for s in range(2)]
        emb = [sb(f"emb{s}", [P, N * D]) for s in range(2)]
        emb_t = [sb(f"emb_t{s}", [P, TP * P]) for s in range(2)]
        junk = [sb(f"junk{s}", [P, 2 * PP, E]) for s in range(2)]
        proj_ss = [sb(f"proj_ss{s}", [P, 2 * PP]) for s in range(2)]
        proj_sd = [sb(f"proj_sd{s}", [P, 2 * PP]) for s in range(2)]
        proj_rs = [sb(f"proj_rs{s}", [P, 2 * PP]) for s in range(2)]
        normed = [sb(f"normed{s}", [P, N, E]) for s in range(2)]
        by_group = [sb(f"by_group{s}", [QN + 1, G, E]) for s in range(2)]
        z_sq = [sb(f"z_sq{s}", [P, UR, PR]) for s in range(2)]
        z_var = [sb(f"z_var{s}", [P, UR]) for s in range(2)]
        z_sd = [sb(f"z_sd{s}", [P, UR]) for s in range(2)]
        z_rs = [sb(f"z_rs{s}", [P, UR]) for s in range(2)]
        z_n = [sb(f"z_n{s}", [P, UR, PR]) for s in range(2)]
        items = [sb(f"items{s}", [P, UR, PR + 1]) for s in range(4)]
        pairs = [sb(f"pairs{s}", [P, JJ, P]) for s in range(2)]
        pair_c = sb("pair_c", [P, OC, P])
        pair_sq = sb("pair_sq", [P, OC, P])
        pair_sd = sb("pair_sd", [P, 1])
        pair_rs = sb("pair_rs", [P, 1])
        rstd_diag = sb("rstd_diag", [P, P])
        scaled_c = sb("scaled_c", [P, ZC, P])
        hidden0 = sb("hidden0", [P, ZC, P])
        hidden1 = sb("hidden1", [P, H1C, P])
        hidden2 = sb("hidden2", [P, H2C, P])
        x_raw = sb("x_raw", [P, XB])
        x_sq = sb("x_sq", [P, XB])
        x_sd = sb("x_sd", [P, XB])
        x_rs = sb("x_rs", [P, XB])
        y_cols = sb("y_cols", [P, TILES])
        y_rows = sb("y_rows", [TILES, P])

        emb_t_ps = psum("emb_t_ps", [P, TP * P])
        proj_ps = [psum(f"proj_ps{s}", [P, 2 * PP * E]) for s in range(2)]
        z_ps = [psum(f"z_ps{s}", [P, UR, PR]) for s in range(2)]
        gram_ps = [psum(f"gram_ps{s}", [P, G // 2, PR]) for s in range(2)]
        top_ps = psum("top_ps", [P, OC, P])
        top_flat = top_ps[:, :, :].rearrange("p a b -> p (a b)")

        weights_in = sem("weights_in")
        dense_in = sem("dense_in")
        late_in = sem("late_in")
        bias_row_in = sem("bias_row_in")
        consts_set = sem("consts_set")
        prep_done = sem("prep_done")
        prep_read = sem("prep_read")
        centred = sem("centred")
        x_scaled = sem("x_scaled")
        ids_in = [sem(f"ids_in{s}") for s in range(2)]
        gathered = [[sem(f"gathered{s}_{c}") for c in range(TCH)] for s in range(2)]
        stored = [sem(f"stored{s}") for s in range(2)]
        loaded = [[sem(f"loaded{s}_{h}") for h in range(2)] for s in range(2)]
        transposed = sem("transposed")
        emb_t_ready = sem("emb_t_ready")
        projected = sem("projected")
        proj_sq = sem("proj_sq")
        proj_std = sem("proj_std")
        proj_rstd = sem("proj_rstd")
        scaled = sem("scaled")
        compressed = sem("compressed")
        squared = sem("squared")
        var_ready = sem("var_ready")
        z_std = sem("z_std")
        z_rstd = sem("z_rstd")
        z_read = sem("z_read")
        z_scaled = sem("z_scaled")
        items_ready = sem("items_ready")
        x_placed = sem("x_placed")
        paired = sem("paired")
        regrouped = sem("regrouped")
        top_done = sem("top_done")
        top_read = sem("top_read")
        rstd_step = sem("rstd_step")
        pool_turn = sem("pool_turn")
        y_read = sem("y_read")
        y_out = sem("y_out")

        C = CREDIT
        block = ctx.enter_context(nc.Block())

        def pairs_in(chunk, size):
            return min(size, NPAIR - chunk * size)

        @block.sync
        def _(sp):
            ids_v = ids.rearrange("(t p) n -> t p n", p=P)

            def load_ids(t, s, c):
                cut = slice(2 * TP * c, min(2 * TP * (c + 1), N))
                sp.dma_start(idx[s][:, cut], ids_v[bass.ds(t, 1), :, cut].rearrange("a p n -> (a p) n")).then_inc(ids_in[s], 16)

            for s in range(2):
                for c in range(TCH):
                    load_ids(s, s, c)
            for s in range(2):
                sp.sem_inc(stored[s], 16)
            sp.dma_start(ws2[:, :], ws_t2).then_inc(weights_in, 16)
            sp.dma_start(ident_sb[:, :], ident).then_inc(weights_in, 16)
            sp.dma_start(wd[:, :, :], wd_t.rearrange("(c p) e -> p c e", p=P)).then_inc(weights_in, 16)
            sp.dma_start(wsi4[:, :], wsi_t4).then_inc(weights_in, 16)
            sp.dma_start(mask[:, :], block_mask).then_inc(weights_in, 16)
            sp.dma_start(first[:, :], first_block).then_inc(weights_in, 16)
            sp.dma_start(gs_b[:, :], gs_rows).then_inc(weights_in, 16)
            sp.dma_start(gsi_b[:, :], gsi_rows).then_inc(weights_in, 16)
            sp.dma_start(bsi_b[:, :], bsi_rows).then_inc(weights_in, 16)
            sp.dma_start(cols[:, :], columns).then_inc(weights_in, 16)
            sp.dma_start(dense[:, :, :], dense_t.rearrange("(c p) b -> p c b", p=P)).then_inc(dense_in, 16)
            for s in range(2):
                sp.dma_start(by_group[s][QN:QN + 1, :, :], bs_row.rearrange("(a g) e -> a g e", a=1)).then_inc(bias_row_in, 16)
            sp.dma_start(wl[:, :, :], wl_pairs).then_inc(late_in, 16)
            sp.dma_start(w1[:, 0:ZC, :], w_top1[0:ZC * P, :].rearrange("(c p) h -> p c h", p=P)).then_inc(late_in, 16)
            sp.dma_start(w1[:, ZC:ZC + FC, :], w_top1[O:O + FD, :].rearrange("(c p) h -> p c h", p=P)).then_inc(late_in, 16)
            sp.dma_start(w2[:, :, :], w_top2.rearrange("(c p) h -> p c h", p=P)).then_inc(late_in, 16)
            sp.wait_ge(prep_read, 1)
            sp.dma_start(wsi_block[QN:QN + 1, :], sum_row[0:1, :]).then_inc(bias_row_in, 16)

            def tile(i, s, more):
                t = 2 * i + s
                if more:
                    for c in range(TCH):
                        sp.wait_ge(gathered[s][c], 32 * pairs_in(c, TP) * (i + 1))
                        load_ids(t + 2, s, c)
                for chunks, cut in ((PCH // 2 + 1, slice(0, N1)), (PCH, slice(N1, N))):
                    sp.wait_ge(scaled, C["scaled"] + PCH * t + chunks)
                    sp.dma_start(scratch[s].rearrange("(p n) e -> p n e", n=N)[:, cut, :],
                                 normed[s][:, cut, :]).then_inc(stored[s], 16)
                sp.wait_ge(stored[s], 32 * (i + 1) + 16)
                sp.wait_ge(compressed, C["compressed"] + UN * (t - 1))
                for h in range(2):
                    sp.dma_start(by_group[s][0:QN, G // 2 * h:G // 2 * (h + 1), :],
                                 scratch[s].rearrange("(g r) e -> r g e", r=QN)[:, G // 2 * h:G // 2 * (h + 1), :]
                                 ).then_inc(loaded[s][h], 16)

            with sp.Fori(0, TILES // 2 - 1) as i:
                tile(i, 0, True)
                tile(i, 1, True)
            tile(TILES // 2 - 1, 0, False)
            tile(TILES // 2 - 1, 1, False)

        @block.gpsimd
        def _(pool):
            with pool.Fori(0, TILES // 2) as i:
                for s in range(2):
                    t = 2 * i + s
                    pool.wait_ge(ids_in[s], 16 * TCH * (i + 1))
                    pool.wait_ge(transposed, C["transposed"] + TCH * (t - 1))
                    pool.sem_inc(pool_turn, 1)
                    for n in range(N):
                        pool.indirect_dma_start(
                            emb[s][:, D * n:D * (n + 1)], None, tables[n][:, :],
                            bass.IndirectOffsetOnAxis(ap=idx[s][:, n:n + 1], axis=0)).then_inc(gathered[s][n // (2 * TP)], 16)

        def regroup_block(s, h, q, jg):
            dst = pairs[s][PR * jg:PR * (jg + 1), :, P // 2 * h + q:P // 2 * (h + 1):Q]
            src = gram_ps[h][PR * q:PR * (q + 1), :, JJ * jg:JJ * (jg + 1)].rearrange("p g j -> p j g")
            return dst, src

        @block.tensor
        def _(pe):
            for name, s in (("transposed", transposed), ("projected", projected), ("compressed", compressed),
                            ("paired", paired)):
                pe.sem_inc(s, C[name])

            def transpose(t, s, c):
                pe.wait_ge(gathered[s][c], 16 * pairs_in(c, TP) * (t - s + 2))
                pe.wait_ge(emb_t_ready, C["emb_t_ready"] + TCH * t + c)
                for a in range(pairs_in(c, TP)):
                    at = 2 * D * (TP * c + a)
                    last = pe.transpose(emb_t_ps[:, P * a:P * (a + 1)], emb[s][:, at:at + 2 * D], ident_sb[:, :])
                last.then_inc(transposed, 1)

            def project(t, s, c):
                if c % 2 == 0:
                    pe.wait_ge(emb_t_ready, C["emb_t_ready"] + TCH * t + c // 2 + 1)
                pe.wait_ge(scaled, PCH * t + c + 1)
                for a in range(pairs_in(c, PP)):
                    at = P * (PP * (c % 2) + a)
                    last = pe.matmul(proj_ps[(s + c) % 2][:, 2 * E * a:2 * E * (a + 1)], emb_t[c // 2 % 2][:, at:at + P],
                                     ws_block[:, :], start=True, stop=True)
                last.then_inc(projected, 1)

            def compress(t, s, m):
                if isinstance(t, int) and t == 0 and m == 0:
                    pe.wait_ge(bias_row_in, 48)
                if m % (UN // 2) == 0:
                    pe.wait_ge(loaded[s][m // (UN // 2)], 8 * (t - s) + 16)
                pe.wait_ge(z_read, UN * t + m + 1)
                for a in range(GU):
                    last = pe.matmul(z_ps[m % 2][:, Q * a:Q * (a + 1), :], by_group[s][:, GU * m + a, :],
                                     wsi_block[:, :], start=True, stop=True)
                last.then_inc(compressed, 1)

            def pair(t, m):
                h = m // (UN // 2)
                if m % (UN // 2) == 0:
                    pe.wait_ge(regrouped, 2 * t + h + 1)
                pe.wait_ge(x_placed, UN * t + m + 1)
                pe.wait_ge(items_ready, UN * t + m + 1)
                it = items[m % 4]
                for a in range(GU):
                    g = GU * (m % (UN // 2)) + a
                    for q in range(Q):
                        r = Q * a + q
                        last = pe.matmul(gram_ps[h][PR * q:PR * (q + 1), g, :], it[:, r, 1:PR + 1], it[:, r, 0:PR],
                                         start=True, stop=True)
                last.then_inc(paired, 1)

            def top(t, s, kind, c):
                if kind == "O":
                    if c == 0 and isinstance(t, int) and t == 0:
                        prologue_over()
                    if c == 0:
                        pe.wait_ge(top_read, C["top_read"] + TOPS * t)
                        pe.wait_ge(regrouped, C["regrouped"] + 2 * t + 2)
                    for jj in range(JJ):
                        last = pe.matmul(top_ps[:, c, :], wl[:, jj, P * c:P * (c + 1)], pairs[s][:, jj, :],
                                         start=jj == 0, stop=jj == JJ - 1)
                    if c == OC - 1:
                        last.then_inc(top_done, 1)
                elif kind == "V":
                    pe.wait_ge(top_read, C["top_read"] + TOPS * t + 1)
                    for oc in range(OC):
                        last = pe.matmul(top_ps[:, 0, 0:1], pair_sq[:, oc, :], ones[:, 0:1], start=oc == 0, stop=oc == OC - 1)
                    last.then_inc(top_done, 1)
                elif kind == "D":
                    pe.wait_ge(rstd_step, 3 * t + 2)
                    pe.matmul(top_ps[:, 0, :], ones[:, :], rstd_diag[:, :], start=True, stop=True).then_inc(top_done, 1)
                elif kind == "A":
                    if c == 0:
                        pe.wait_ge(top_read, C["top_read"] + TOPS * t + 3)
                    for f in range(FC):
                        pe.matmul(top_ps[:, c, :], w1[:, ZC + f, P * c:P * (c + 1)], dense[:, f, bass.ds(P * t, P)],
                                  start=f == 0, stop=False)
                    for o in range(ZC):
                        last = pe.matmul(top_ps[:, c, :], w1[:, o, P * c:P * (c + 1)], hidden0[:, o, :],
                                         start=False, stop=o == ZC - 1)
                    if c == H1C - 1:
                        last.then_inc(top_done, 1)
                elif kind == "B":
                    if c == 0:
                        pe.wait_ge(top_read, C["top_read"] + TOPS * t + 4)
                    for h in range(H1C):
                        last = pe.matmul(top_ps[:, c, :], w2[:, h, P * c:P * (c + 1)], hidden1[:, h, :],
                                         start=h == 0, stop=h == H1C - 1)
                    if c == H2C - 1:
                        last.then_inc(top_done, 1)
                else:
                    pe.wait_ge(top_read, C["top_read"] + TOPS * t + 5)
                    for h in range(H2C):
                        last = pe.matmul(top_ps[:, 0, 0:1], hidden2[:, h, :], col["w3"][h], start=h == 0, stop=h == H2C - 1)
                    last.then_inc(top_done, 1)

            pe.wait_ge(consts_set, 4)
            pe.matmul(top_flat[0:1, 0:P], first[:, :], wsi_c[:, :, :].rearrange("r q p -> r (q p)"),
                      start=True, stop=True).then_inc(prep_done, 1)
            def prologue_over():
                pe.wait_ge(prep_read, 2 * XBLK + 1)
                pe.wait_ge(late_in, 64)
                pe.wait_ge(consts_set, 6)

            def project_x(blk):
                pe.wait_ge(dense_in, 16)
                pe.wait_ge(prep_read, 2 * blk + 1)
                for c in range(FC):
                    last = pe.matmul(top_flat, wd[:, c, :], dense[:, c, XB * blk:XB * (blk + 1)],
                                     start=c == 0, stop=c == FC - 1)
                last.then_inc(prep_done, 1)

            def sum_x_squares(blk):
                pe.wait_ge(prep_read, 2 * blk + 2)
                pe.matmul(top_flat, ones[:, :], x_sq[:, :], start=True, stop=True).then_inc(prep_done, 1)

            def step(t, s):
                for kind, c, lag in items_of(PE_ORDER, t, TILES):
                    tile, slot = t + lag, (s + lag) % 2
                    if kind == "t":
                        transpose(tile, slot, c)
                    elif kind == "p":
                        project(tile, slot, c)
                    elif kind == "z":
                        compress(tile, slot, c)
                    elif kind == "g":
                        pair(tile, c)
                    elif kind == "X":
                        project_x(c)
                    elif kind == "S":
                        sum_x_squares(c)
                    else:
                        top(tile, slot, kind, c)

            for t in range(-2, 2):
                step(t, t % 2)
            if FIRST_TOP == 2:
                prologue_over()
            with pe.Fori(1, TILES // 2 - 1) as i:
                step(2 * i, 0)
                step(2 * i + 1, 1)
            for t in range(TILES - 2, TILES + 2):
                step(t, t % 2)
            pe.wait_ge(top_read, C["top_read"] + TOPS * TILES)
            pe.transpose(top_flat[0:TILES, 0:P], y_cols[:, :], ident_sb[:, :]).then_inc(top_done, 1)

        @block.scalar
        def _(act):
            for name, s in (("emb_t_ready", emb_t_ready), ("regrouped", regrouped), ("top_read", top_read)):
                act.sem_inc(s, C[name])

            def copy_emb_t(t, c):
                act.wait_ge(transposed, C["transposed"] + TCH * t + c + 1)
                before = PCH * t + (2 * c - 2 if c >= 2 else c - 1)
                act.wait_ge(projected, C["projected"] + before)
                w = P * pairs_in(c, TP)
                act.activation(emb_t[c % 2][:, 0:w], emb_t_ps[:, 0:w], ACT.Copy).then_inc(emb_t_ready, 1)

            def square_proj(t, j, c):
                act.wait_ge(projected, C["projected"] + PCH * t + c + 1)
                s = (j + c) % 2
                for a in range(2 * pairs_in(c, PP)):
                    last = act.activation(junk[s][:, a, :], proj_ps[s][:, E * a:E * (a + 1)], ACT.Square,
                                          accum_out=proj_ss[s][:, a:a + 1])
                last.then_inc(proj_sq, 1)

            def std_proj(t, j, c):
                s, w = (j + c) % 2, 2 * pairs_in(c, PP)
                act.wait_ge(proj_sq, PCH * t + c + 1)
                act.activation(proj_sd[s][:, 0:w], proj_ss[s][:, 0:w], ACT.Sqrt, bias=eps[:, :],
                               scale=1.0 / E).then_inc(proj_std, 1)

            def square_z(t, m):
                act.wait_ge(compressed, C["compressed"] + UN * t + m + 1)
                act.wait_ge(var_ready, UN * t + m + 1)
                act.activation(z_sq[m % 2][:, :, :], z_ps[m % 2][:, :, :], ACT.Square).then_inc(squared, 1)

            def std_z(t, m):
                act.wait_ge(var_ready, C["var_ready"] + UN * t + m + 1)
                act.activation(z_sd[m % 2][:, :], z_var[m % 2][:, :], ACT.Sqrt, bias=eps[:, :],
                               scale=1.0 / PR).then_inc(z_std, 1)

            def place_x(t, m):
                if isinstance(t, int) and t == 0 and m == 0:
                    act.wait_ge(x_scaled, 4 * XBLK)
                act.wait_ge(paired, UN * t + m + 1)
                act.activation(items[m % 4][:, :, 0], x_all[:, bass.ds(P * t + UR * m, UR)], ACT.Copy).then_inc(x_placed, 1)

            def regroup(t, s, h):
                act.wait_ge(paired, C["paired"] + UN * t + UN // 2 * (h + 1))
                for q in range(Q):
                    for jg in range(Q):
                        last = act.activation(*regroup_block(s, h, q, jg), ACT.Copy)
                last.then_inc(regrouped, 1)

            def top(t, kind):
                def done(k):
                    act.wait_ge(top_done, TOPS * t + k)

                if kind == "O":
                    done(1)
                    act.activation(pair_c[:, :, :], top_ps[:, :, :], ACT.Copy)
                    act.activation(pair_sq[:, :, :], top_ps[:, :, :], ACT.Square).then_inc(top_read, 1)
                elif kind == "V":
                    done(2)
                    act.activation(pair_sd[:, :], top_ps[:, 0, 0:1], ACT.Sqrt, bias=eps[:, :],
                                   scale=1.0 / O).then_inc(top_read, 1)
                elif kind == "H":
                    act.wait_ge(rstd_step, 3 * t + 3)
                    for c in range(ZC):
                        last = act.activation(hidden0[:, c, :], scaled_c[:, c, :], ACT.Identity, bias=col["bl"][c],
                                              scale=col["gl"][c])
                    last.then_inc(top_read, 1)
                elif kind == "A":
                    done(4)
                    for h in range(H1C):
                        last = act.activation(hidden1[:, h, :], top_ps[:, h, :], ACT.Relu, bias=col["b1"][h])
                    last.then_inc(top_read, 1)
                elif kind == "B":
                    done(5)
                    for h in range(H2C):
                        last = act.activation(hidden2[:, h, :], top_ps[:, h, :], ACT.Relu, bias=col["b2"][h])
                    last.then_inc(top_read, 1)
                else:
                    done(6)
                    act.activation(y_cols[:, bass.ds(t, 1)], top_ps[:, 0, 0:1], ACT.Copy).then_inc(top_read, 1)

            act.wait_ge(consts_set, 3)
            act.wait_ge(prep_done, 1)
            act.activation(sum_row[:, :], top_flat[0:1, 0:P], ACT.Copy).then_inc(prep_read, 1)

            def read_x(blk):
                act.wait_ge(prep_done, 2 * blk + 2)
                if blk >= 1:
                    act.wait_ge(x_scaled, 4 * blk)
                act.activation(x_raw[:, :], top_flat, ACT.Copy)
                act.activation(x_sq[:, :], top_flat, ACT.Square).then_inc(prep_read, 1)

            def std_x(blk):
                act.wait_ge(prep_done, 2 * blk + 3)
                act.activation(x_sd[:, :], top_flat, ACT.Sqrt, bias=eps[:, :], scale=1.0 / E).then_inc(prep_read, 1)

            def step(t, s):
                for kind, c, lag in items_of(ACT_ORDER, t, TILES):
                    tile, slot = t + lag, (s + lag) % 2
                    if kind == "t":
                        copy_emb_t(tile, c)
                    elif kind == "p":
                        square_proj(tile, slot, c)
                        std_proj(tile, slot, c)
                    elif kind == "z":
                        square_z(tile, c)
                    elif kind == "v":
                        std_z(tile, c)
                    elif kind == "x":
                        place_x(tile, c)
                    elif kind == "r":
                        regroup(tile, slot, c)
                    elif kind == "X":
                        read_x(c)
                    elif kind == "S":
                        std_x(c)
                    else:
                        top(tile, kind)

            for t in range(-2, 2):
                step(t, t % 2)
            with act.Fori(1, TILES // 2 - 1) as i:
                step(2 * i, 0)
                step(2 * i + 1, 1)
            for t in range(TILES - 2, TILES + 2):
                step(t, t % 2)
            act.wait_ge(top_done, TOPS * TILES + 1)
            act.activation(y_rows[:, :], top_flat[0:TILES, 0:P], ACT.Copy).then_inc(y_read, 1)
            act.wait_ge(y_read, 1)
            act.dma_start(out.rearrange("(t p) a -> t (p a)", p=P), y_rows[:, :]).then_inc(y_out, 16)
            act.wait_ge(y_out, 16)

        @block.vector
        def _(dve):
            for name, s in (("scaled", scaled), ("var_ready", var_ready), ("z_read", z_read)):
                dve.sem_inc(s, C[name])
            dve.memset(ones[:, :], 1.0)
            dve.memset(eps[:, :], EPS)
            dve.memset(ws_block[:, :], 0.0).then_inc(consts_set, 1)
            dve.wait_ge(weights_in, 16 * 10)

            def centre(dst, src, mean, width, step):
                dve.tensor_reduce(mean, src, AX_X, ALU.add).then_inc(centred, 1)
                dve.wait_ge(centred, step)
                dve.tensor_scalar(mean, mean, 1.0 / width, None, ALU.mult).then_inc(centred, 1)
                dve.wait_ge(centred, step + 1)
                return dve.tensor_tensor(dst, src, mean.to_broadcast(list(src.shape)) if mean.ndim == src.ndim
                                         else mean.unsqueeze(mean.ndim).to_broadcast(list(src.shape)), ALU.subtract)

            dve.wait_ge(consts_set, 1)
            centre(ws2[:, :], ws2[:, :], means[:, 0:1], E, 1).then_inc(centred, 1)
            dve.wait_ge(centred, 3)
            for s in range(2):
                last = dve.tensor_copy(ws_block[D * s:D * (s + 1), E * s:E * (s + 1)], ws2[D * s:D * (s + 1), :])
            last.then_inc(consts_set, 1)
            centre(wd[:, :, :], wd[:, :, :], means[:, 2:2 + FC], E, 4).then_inc(consts_set, 1)
            centre(wsi4[:, :], wsi4[:, :], means[0:QN, 1:2], PR, 6).then_inc(centred, 1)
            dve.wait_ge(centred, 8)
            for q in range(Q):
                dve.tensor_copy(wsi_c[:, q, :], wsi4[:, :])
                last = dve.tensor_scalar(wsi_block[0:QN, PR * q:PR * (q + 1)], wsi4[:, :], mask[:, q:q + 1], None, ALU.mult)
            last.then_inc(consts_set, 1)

            def recip_proj(t, j, c):
                s, w = (j + c) % 2, 2 * pairs_in(c, PP)
                dve.wait_ge(proj_std, PCH * t + c + 1)
                dve.reciprocal(proj_rs[s][:, 0:w], proj_sd[s][:, 0:w]).then_inc(proj_rstd, 1)

            def scale_proj(t, j, c):
                s = (j + c) % 2
                if c == 0:
                    dve.wait_ge(stored[j], 16 * (t - j) + 16)
                dve.wait_ge(proj_rstd, PCH * t + c + 1)
                for a in range(2 * pairs_in(c, PP)):
                    last = dve.scalar_tensor_tensor(
                        out=normed[j][:, 2 * PP * c + a, :], in0=proj_ps[s][:, E * a:E * (a + 1)],
                        scalar=proj_rs[s][:, a:a + 1], in1=gs_b[:, :], op0=ALU.mult, op1=ALU.mult)
                last.then_inc(scaled, 1)

            def reduce_z(t, m):
                dve.wait_ge(squared, UN * t + m + 1)
                dve.tensor_reduce(z_var[m % 2][:, :], z_sq[m % 2][:, :, :], AX_X, ALU.add).then_inc(var_ready, 1)

            def recip_z(t, m):
                dve.wait_ge(z_std, UN * t + m + 1)
                dve.reciprocal(z_rs[m % 2][:, :], z_sd[m % 2][:, :]).then_inc(z_rstd, 1)

            def scale_z(t, m):
                dve.wait_ge(z_rstd, UN * t + m + 1)
                dve.tensor_tensor(z_n[m % 2][:, :, :], z_ps[m % 2][:, :, :],
                                  z_rs[m % 2][:, :].unsqueeze(2).to_broadcast([P, UR, PR]), ALU.mult).then_inc(z_read, 1)

            def times_gsi(t, m):
                dve.wait_ge(z_read, C["z_read"] + UN * t + m + 1)
                dve.tensor_tensor(z_n[m % 2][:, :, :], z_n[m % 2][:, :, :],
                                  gsi_b[:, :].unsqueeze(1).to_broadcast([P, UR, PR]), ALU.mult).then_inc(z_scaled, 1)

            def fill_items(t, m):
                dve.wait_ge(paired, UN * t + m + 1)
                dve.wait_ge(z_scaled, UN * t + m + 1)
                dve.tensor_tensor(items[m % 4][:, :, 1:PR + 1], z_n[m % 2][:, :, :],
                                  bsi_b[:, :].unsqueeze(1).to_broadcast([P, UR, PR]), ALU.add).then_inc(items_ready, 1)

            def norm_x(blk):
                xs = x_all[:, XB * blk:XB * (blk + 1)]
                dve.wait_ge(prep_read, 2 * blk + 3)
                dve.reciprocal(x_rs[:, :], x_sd[:, :]).then_inc(x_scaled, 1)
                dve.wait_ge(x_scaled, 4 * blk + 1)
                dve.tensor_tensor(xs, x_raw[:, :], x_rs[:, :], ALU.mult).then_inc(x_scaled, 1)
                dve.wait_ge(x_scaled, 4 * blk + 2)
                dve.tensor_scalar(xs, xs, col["gd"][0], col["bd"][0], ALU.mult, ALU.add).then_inc(x_scaled, 2)

            def centre_wl():
                dve.wait_ge(late_in, 64)
                centre(wl[:, :, :], wl[:, :, :], means[:, 2 + FC:2 + FC + JJ], O, 9).then_inc(consts_set, 2)

            def spread_rstd(t):
                dve.wait_ge(top_read, C["top_read"] + TOPS * t + 2)
                dve.reciprocal(pair_rs[:, :], pair_sd[:, :]).then_inc(rstd_step, 1)
                dve.wait_ge(rstd_step, 3 * t + 1)
                dve.tensor_scalar(rstd_diag[:, :], ident_sb[:, :], pair_rs[:, 0:1], None, ALU.mult).then_inc(rstd_step, 1)

            def scale_pairs(t):
                dve.wait_ge(top_done, TOPS * t + 3)
                dve.tensor_tensor(scaled_c[:, :, :], pair_c[:, 0:ZC, :],
                                  top_ps[:, 0, :].unsqueeze(1).to_broadcast([P, ZC, P]), ALU.mult).then_inc(rstd_step, 1)

            def step(t, s):
                for kind, c, lag in items_of(DVE_ORDER, t, TILES):
                    tile, slot = t + lag, (s + lag) % 2
                    if kind == "p":
                        recip_proj(tile, slot, c)
                        scale_proj(tile, slot, c)
                    elif kind == "z":
                        reduce_z(tile, c)
                    elif kind == "R":
                        recip_z(tile, c)
                    elif kind == "M":
                        scale_z(tile, c)
                    elif kind == "G":
                        times_gsi(tile, c)
                    elif kind == "a":
                        fill_items(tile, c)
                    elif kind == "X":
                        norm_x(c)
                    elif kind == "W":
                        centre_wl()
                    elif kind == "V":
                        spread_rstd(tile)
                    else:
                        scale_pairs(tile)

            for t in range(-2, 2):
                step(t, t % 2)
            with dve.Fori(1, TILES // 2 - 1) as i:
                step(2 * i, 0)
                step(2 * i + 1, 1)
            for t in range(TILES - 2, TILES + 2):
                step(t, t % 2)


def kernel(**inputs):
    import numpy as np
    import concourse.bacc as bacc
    from concourse.bass_utils import run_bass_kernel_spmd

    a = {k: np.ascontiguousarray(v) for k, v in inputs.items()}
    N, D = 26, 64
    E = a["L0_rec_Wd"].shape[0]
    PR = a["L0_rec_Wsi"].shape[0]
    O = a["L0_rec_Wl"].shape[0]
    Q, JJ = 128 // PR, PR // (128 // PR)

    def columns(v):
        return v.reshape(-1, 128).T

    wl = np.zeros((Q, PR, JJ, O), np.float32)
    wl_t = a["L0_rec_Wl"].T
    for p in range(PR):
        for j in range(p + 1):
            wl[j // JJ, p, j % JJ] = wl_t[p * (p + 1) // 2 + j]
    arrays = {"ids": a["ids"]}
    for n in range(N):
        arrays[f"tbl_{n}"] = a[f"tbl_{n}"]
    arrays.update(
        dense_t=a["r_dense_t"].T,
        ident=np.eye(128, dtype=np.float32),
        wd_t=a["L0_rec_Wd"].T,
        ws_t2=np.concatenate([a["L0_rec_Ws"].T] * 2, axis=0),
        wsi_t4=np.concatenate([a["L0_rec_Wsi"].T] * Q, axis=0),
        block_mask=np.repeat(np.eye(Q, dtype=np.float32), N, axis=0),
        first_block=np.repeat(np.eye(Q, dtype=np.float32)[:, 0:1], N, axis=0),
        bs_row=np.tile(a["L0_rec_bs"], (128 // Q, 1)),
        gs_rows=np.tile(a["L0_rec_gs"], (128, 1)),
        gsi_rows=np.tile(a["L0_rec_gsi"], (128, 1)),
        bsi_rows=np.tile(a["L0_rec_bsi"], (128, 1)),
        columns=np.concatenate([columns(a[k]) for k in ("L0_rec_gd", "L0_rec_bd", "L0_rec_gl", "L0_rec_bl",
                                                        "b_top1", "b_top2")] + [columns(a["W_top3"][:, 0])], axis=1),
        wl_pairs=wl.reshape(128, JJ, O),
        w_top1=a["W_top1"],
        w_top2=a["W_top2"],
    )
    arrays = {f"in_{k}": np.ascontiguousarray(v) for k, v in arrays.items()}
    nc = bacc.Bacc("TRN2", target_bir_lowering=False, num_devices=1)
    aps = [nc.dram_tensor(k, v.shape, mybir.dt.from_np(v.dtype), kind="ExternalInput").ap() for k, v in arrays.items()]
    out = nc.dram_tensor("out_y", (a["ids"].shape[0], 1), mybir.dt.float32, kind="ExternalOutput").ap()
    dlrm_tower(nc, aps[0], aps[1:1 + N], *aps[1 + N:], out)
    r = run_bass_kernel_spmd(nc, [arrays], core_ids=[0])
    return r.results[0]["out_y"]
```
